# Optimizing a Trainium2 kernel written in Bass

```python
import numpy as np
import jax
import jax.numpy as jnp

def _softmax(x, axis=-1):
    return jax.nn.softmax(x, axis=axis)

def _gelu(x):
    return jax.nn.gelu(x, approximate=True)

def _silu(x):
    return jax.nn.silu(x)

def _sigmoid(x):
    return jax.nn.sigmoid(x)

def _layernorm(x, axis=-1, eps=1e-05):
    m = jnp.mean(x, axis=axis, keepdims=True)
    v = jnp.var(x, axis=axis, keepdims=True)
    return (x - m) / jnp.sqrt(v + eps)

def _scatter_add(tgt, idx, src, axis=0):
    return tgt.at[idx].add(src)

def _segment_sum(src, seg, n):
    return jax.ops.segment_sum(src, seg, n)
kernel_name = 'mk_conv_attn_hybrid_d2_conv_nchw128_r4_2dc75a'

def setup_inputs(seed: int=0):
    np.random.seed(seed)
    _w = jnp.asarray

    def _rec_inputs():
        import jax
        import jax.numpy as jnp
        _gk = jax.random.key(seed)
        x = -0.0005207 + 1.001 * jax.random.normal(jax.random.fold_in(_gk, 1), (4, 32, 16, 16), jnp.float32)
        return x
    x = _rec_inputs()

    def _L0_conv_setup():
        import jax, jax.numpy as jnp
        import numpy as np
        THRESHOLD = 16.0
        BN_EPS = 1e-05
        key = jax.random.key(seed)
        k_x, k_w, k_b, k_g, k_be = jax.random.split(key, 5)
        B, C, H, W = (4, 32, 16, 16)
        C2 = 32
        x = jax.random.normal(k_x, (B, C, H, W), dtype=jnp.float32)
        W_fc = jax.random.normal(k_w, (C2, C), dtype=jnp.float32) * (1.0 / np.sqrt(C))
        b_fc = jax.random.normal(k_b, (C2,), dtype=jnp.float32) * 0.01
        gamma = jnp.ones((C2,), dtype=jnp.float32) + 0.1 * jax.random.normal(k_g, (C2,), dtype=jnp.float32)
        beta = 0.1 * jax.random.normal(k_be, (C2,), dtype=jnp.float32)
        return {'x': x, 'W_fc': W_fc, 'b_fc': b_fc, 'gamma': gamma, 'beta': beta}
    _L0_conv_all = _L0_conv_setup()
    _L0_conv_in = {k: v for k, v in _L0_conv_all.items() if k in ('W_fc', 'b_fc', 'gamma', 'beta')}
    del _L0_conv_all

    def _L1_attn_setup():
        import jax, jax.numpy as jnp
        import numpy as np
        key = jax.random.key(seed)
        x = jax.random.normal(key, (4, 1024, 32), dtype=jnp.float32)
        return {'x': x}
    _L1_attn_all = _L1_attn_setup()
    _L1_attn_in = {k: v for k, v in _L1_attn_all.items() if k in ()}
    del _L1_attn_all

    def _L1_ffn_setup():
        import jax, jax.numpy as jnp
        import numpy as np
        PADDED_SL = 2048
        TEMPERATURE = 1.0
        SIGMA_POW = 0.25

        def _stu_conv(phi, u, n):
            b, sl, d = u.shape
            sgn = jnp.where(jnp.arange(sl) % 2 == 0, 1.0, -1.0).astype(u.dtype)
            sgn3 = sgn[None, :, None]
            Vf = jnp.fft.rfft(phi, n=n, axis=0)
            Uf_p = jnp.fft.rfft(u, n=n, axis=1)
            Uf_m = jnp.fft.rfft(u * sgn3, n=n, axis=1)
            U_plus = jnp.fft.irfft(Vf[None, :, :, None] * Uf_p[:, :, None, :], n=n, axis=1)[:, :sl]
            U_minus = jnp.fft.irfft(Vf[None, :, :, None] * Uf_m[:, :, None, :], n=n, axis=1)[:, :sl]
            U_minus = U_minus * sgn[None, :, None, None]
            return (U_plus, U_minus)

        def _compute_spectral(u, sigma, phi, Mpp, Mpm):
            U_plus, U_minus = _stu_conv(phi, u, PADDED_SL)
            s = sigma ** SIGMA_POW
            out = jnp.einsum('btkd,k,kde->bte', U_plus, s, Mpp)
            out = out + jnp.einsum('btkd,k,kde->bte', U_minus, s, Mpm)
            return out

        def _compute_ar_u(Mu, u):
            sl = u.shape[1]
            out = jnp.zeros(u.shape[:2] + (Mu.shape[-1],), dtype=u.dtype)
            for i in range(Mu.shape[0]):
                ui = jnp.pad(u, ((0, 0), (i, 0), (0, 0)))[:, :sl]
                out = out + jnp.einsum('btd,de->bte', ui, Mu[i])
            return out

        def _stu(u, sigma, phi, Mu, Mpp, Mpm):
            return _compute_spectral(u, sigma, phi, Mpp, Mpm) + _compute_ar_u(Mu, u)
        key = jax.random.key(seed)
        ks = jax.random.split(key, 8)
        b, sl, d, K, k_u = (2, 1024, 32, 16, 3)
        x = jax.random.normal(ks[0], (b, sl, d), dtype=jnp.float32)
        sigma = jax.random.uniform(ks[1], (K,), dtype=jnp.float32, minval=0.001, maxval=1.0)
        phi = jax.random.normal(ks[2], (sl, K), dtype=jnp.float32) / np.sqrt(sl)
        M_u = jax.random.normal(ks[3], (4, k_u, d, d), dtype=jnp.float32) * 0.02
        M_phi_plus = jax.random.normal(ks[4], (4, K, d, d), dtype=jnp.float32) * 0.02
        M_phi_minus = jax.random.normal(ks[5], (4, K, d, d), dtype=jnp.float32) * 0.02
        log_weights = jnp.ones((4,), dtype=jnp.float32)
        u01 = jax.random.uniform(ks[6], (4,), dtype=jnp.float32, minval=1e-06, maxval=1.0 - 1e-06)
        gumbel = -jnp.log(-jnp.log(u01))
        return {'x': x, 'sigma': sigma, 'phi': phi, 'M_u': M_u, 'M_phi_plus': M_phi_plus, 'M_phi_minus': M_phi_minus, 'log_weights': log_weights, 'gumbel': gumbel}
    _L1_ffn_all = _L1_ffn_setup()
    _L1_ffn_in = {k: v for k, v in _L1_ffn_all.items() if k in ('sigma', 'phi', 'M_u', 'M_phi_plus', 'M_phi_minus', 'log_weights', 'gumbel')}
    del _L1_ffn_all
    return {'x': x, 'L0_conv_W_fc': _L0_conv_in['W_fc'], 'L0_conv_b_fc': _L0_conv_in['b_fc'], 'L0_conv_gamma': _L0_conv_in['gamma'], 'L0_conv_beta': _L0_conv_in['beta'], 'L1_ffn_sigma': _L1_ffn_in['sigma'], 'L1_ffn_phi': _L1_ffn_in['phi'], 'L1_ffn_M_u': _L1_ffn_in['M_u'], 'L1_ffn_M_phi_plus': _L1_ffn_in['M_phi_plus'], 'L1_ffn_M_phi_minus': _L1_ffn_in['M_phi_minus'], 'L1_ffn_log_weights': _L1_ffn_in['log_weights'], 'L1_ffn_gumbel': _L1_ffn_in['gumbel']}

def reference(x, L0_conv_W_fc, L0_conv_b_fc, L0_conv_gamma, L0_conv_beta, L1_ffn_sigma, L1_ffn_phi, L1_ffn_M_u, L1_ffn_M_phi_plus, L1_ffn_M_phi_minus, L1_ffn_log_weights, L1_ffn_gumbel):
    import jax
    import jax.numpy as jnp

    def _L0_conv_ref(x, W_fc, b_fc, gamma, beta):
        import jax, jax.numpy as jnp
        import numpy as np
        THRESHOLD = 16.0
        BN_EPS = 1e-05
        b, c, h, w = x.shape
        xf = x.reshape(b, c, h * w).transpose(0, 2, 1)
        sq = jnp.sum(xf * xf, axis=-1)
        d2 = sq[:, :, None] + sq[:, None, :] - 2.0 * jnp.einsum('bic,bjc->bij', xf, xf)
        dist = jnp.sqrt(jnp.maximum(d2, 0.0))
        incidence = (dist < THRESHOLD).astype(x.dtype)
        xe = jnp.einsum('bnc,dc->bnd', xf, W_fc) + b_fc
        deg_e = jnp.sum(incidence, axis=1)
        edge = jnp.einsum('bve,bvc->bec', incidence, xe)
        edge = jnp.where(deg_e > 0, 1.0 / deg_e, 0.0)[:, :, None] * edge
        deg_v = jnp.sum(incidence, axis=2)
        vert = jnp.einsum('bve,bec->bvc', incidence, edge)
        vert = jnp.where(deg_v > 0, 1.0 / deg_v, 0.0)[:, :, None] * vert
        out = vert + xf
        out = out.transpose(0, 2, 1).reshape(b, -1, h, w)
        mean = jnp.mean(out, axis=(0, 2, 3))
        var = jnp.var(out, axis=(0, 2, 3))
        y = (out - mean[None, :, None, None]) * jax.lax.rsqrt(var[None, :, None, None] + BN_EPS)
        y = gamma[None, :, None, None] * y + beta[None, :, None, None]
        return y * jax.nn.sigmoid(y)

    def _L1_attn_ref(x):
        import jax, jax.numpy as jnp
        import numpy as np
        scores = jnp.einsum('bsd,btd->bst', x, x)
        attn_weights = jax.nn.softmax(scores, axis=-1)
        return jnp.einsum('bst,btd->bsd', attn_weights, x)

    def _L1_ffn_ref(x, sigma, phi, M_u, M_phi_plus, M_phi_minus, log_weights, gumbel):
        import jax, jax.numpy as jnp
        import numpy as np
        PADDED_SL = 2048
        TEMPERATURE = 1.0
        SIGMA_POW = 0.25

        def _stu_conv(phi, u, n):
            b, sl, d = u.shape
            sgn = jnp.where(jnp.arange(sl) % 2 == 0, 1.0, -1.0).astype(u.dtype)
            sgn3 = sgn[None, :, None]
            Vf = jnp.fft.rfft(phi, n=n, axis=0)
            Uf_p = jnp.fft.rfft(u, n=n, axis=1)
            Uf_m = jnp.fft.rfft(u * sgn3, n=n, axis=1)
            U_plus = jnp.fft.irfft(Vf[None, :, :, None] * Uf_p[:, :, None, :], n=n, axis=1)[:, :sl]
            U_minus = jnp.fft.irfft(Vf[None, :, :, None] * Uf_m[:, :, None, :], n=n, axis=1)[:, :sl]
            U_minus = U_minus * sgn[None, :, None, None]
            return (U_plus, U_minus)

        def _compute_spectral(u, sigma, phi, Mpp, Mpm):
            U_plus, U_minus = _stu_conv(phi, u, PADDED_SL)
            s = sigma ** SIGMA_POW
            out = jnp.einsum('btkd,k,kde->bte', U_plus, s, Mpp)
            out = out + jnp.einsum('btkd,k,kde->bte', U_minus, s, Mpm)
            return out

        def _compute_ar_u(Mu, u):
            sl = u.shape[1]
            out = jnp.zeros(u.shape[:2] + (Mu.shape[-1],), dtype=u.dtype)
            for i in range(Mu.shape[0]):
                ui = jnp.pad(u, ((0, 0), (i, 0), (0, 0)))[:, :sl]
                out = out + jnp.einsum('btd,de->bte', ui, Mu[i])
            return out

        def _stu(u, sigma, phi, Mu, Mpp, Mpm):
            return _compute_spectral(u, sigma, phi, Mpp, Mpm) + _compute_ar_u(Mu, u)
        T = x.shape[1]
        outs = []
        for i, frac in enumerate((1, 2, 4, 8)):
            xi = x[:, :T // frac]
            si = _stu(xi, sigma, phi, M_u[i], M_phi_plus[i], M_phi_minus[i])
            si = jnp.pad(si, ((0, 0), (0, T - si.shape[1]), (0, 0)))
            outs.append(si)
        y_soft = jax.nn.softmax((log_weights + gumbel) / TEMPERATURE)
        y_hard = jax.nn.one_hot(jnp.argmax(y_soft), 4, dtype=y_soft.dtype)
        weights = y_hard - jax.lax.stop_gradient(y_soft) + y_soft
        stacked = jnp.stack(outs, axis=-1)
        return jnp.sum(stacked * weights, axis=-1)

    def _gn(v, G=32, eps=1e-05):
        B_, C_, H_, W_ = v.shape
        g = v.reshape(B_, G, C_ // G, H_, W_)
        m = jnp.mean(g, axis=(2, 3, 4), keepdims=True)
        s = jnp.var(g, axis=(2, 3, 4), keepdims=True)
        return ((g - m) / jnp.sqrt(s + eps)).reshape(v.shape)

    def _ln_c(v, eps=1e-06):
        m = jnp.mean(v, axis=1, keepdims=True)
        s = jnp.var(v, axis=1, keepdims=True)
        return (v - m) / jnp.sqrt(s + eps)

    def _ln_t(v, eps=1e-05):
        m = jnp.mean(v, axis=-1, keepdims=True)
        s = jnp.var(v, axis=-1, keepdims=True)
        return (v - m) / jnp.sqrt(s + eps)

    def _to_tokens(v):
        B_, C_, H_, W_ = v.shape
        return v.reshape(B_, C_, H_ * W_).transpose(0, 2, 1)

    def _from_tokens(t, like):
        B_, C_, H_, W_ = like.shape
        return t.transpose(0, 2, 1).reshape(B_, C_, H_, W_)
    x = x + _L0_conv_ref(_gn(x), L0_conv_W_fc, L0_conv_b_fc, L0_conv_gamma, L0_conv_beta)
    t = _to_tokens(x)
    t = t + _L1_attn_ref(_ln_t(t))
    t = t + _L1_ffn_ref(_ln_t(t), L1_ffn_sigma, L1_ffn_phi, L1_ffn_M_u, L1_ffn_M_phi_plus, L1_ffn_M_phi_minus, L1_ffn_log_weights, L1_ffn_gumbel)
    x = _from_tokens(t, x)
    return x

_drawn_inputs = setup_inputs


def setup_inputs(seed=0):
    import zlib

    import numpy as np

    out = dict(_drawn_inputs(seed))
    spreads = {'L1_ffn_log_weights': (1.0, 0.2)}
    factors = {'L0_conv_W_fc': 8.0, 'L0_conv_b_fc': 8.0, 'L1_ffn_sigma': 2.881}
    for name, (base, spread) in spreads.items():
        noise = np.random.default_rng([zlib.crc32(name.encode()), seed]).standard_normal(out[name].shape)
        drawn = base * np.exp(spread * noise) if base else spread * noise
        out[name] = jnp.asarray(drawn.astype(out[name].dtype))
    for name, factor in factors.items():
        out[name] = (out[name] * factor).astype(out[name].dtype)
    return out
```

```python
from contextlib import ExitStack

import numpy as np

import concourse.bass as bass
from concourse import mybir

ALU = mybir.AluOpType
ACT = mybir.ActivationFunctionType
F32 = mybir.dt.float32
F16 = mybir.dt.float16
I32 = mybir.dt.int32
AX_X = mybir.AxisListType.X
RMAX = bass.bass_isa.ReduceOp.max

B, C, T = 4, 32, 256
P = B * C
HT = T // 2
NX = 4
K = 16
NTAU = 3
PH = P // C
T4 = T // PH
NPAIR = C // 2
BN_EPS = 1e-5
GN_EPS = 1e-5
LN_EPS = 1e-5
RADIUS2 = 16.0 ** 2
USCALE = 256.0
GTOP = 2.0 ** 13

IDENT, CENTER_BD, CENTER_ALL, SAME_C, REP_K = (n * P for n in range(5))
SIGN = 5 * P
COL32 = SIGN + T
COLHALF = COL32 + B
EXPERT = COLHALF + B
BMASK = EXPERT + NX
TMASK = BMASK + B * 6
FIRST = TMASK + NX * T
NCONST = FIRST + NX
P_WT, P_BIAS, P_GAMMA, P_BETA, P_SIGMA, P_LOGW, P_GUMBEL = 0, P, 2 * P, 2 * P + 1, 2 * P + 2, 2 * P + 3, 2 * P + 7
NSMALL = P_GUMBEL + NX

SPOTS = dict(gram=0, compare=2, edge=2, vert=2, bn=2, silu=2, ln1=2, scores=2, av=2, ln2=0)


def stu_hybrid_kernel(nc, x, consts, small, mfilt, phi4, mu4, out):
    with ExitStack() as ctx:
        def sb(name, shape, dt=F32):
            return ctx.enter_context(nc.sbuf_tensor(name, shape, dt))

        sems = {}

        def sem(name):
            if name not in sems:
                sems[name] = ctx.enter_context(nc.semaphore("s_" + name))
            return sems[name]

        bank = [ctx.enter_context(nc.psum_tensor(f"bank{i}", [P, 512], F32)) for i in range(4)]
        quad = ctx.enter_context(nc.psum_tensor("quad", [P, 4, 512], F32))
        chainA, chainB, gbank = bank[0], bank[1], bank[2:4]

        x_sb = sb("x_sb", [P, T])
        cst = sb("cst", [P, NCONST])
        sml = sb("sml", [P, NSMALL])
        m_sb = sb("m_sb", [P, C * C])
        phi_sb = sb("phi_sb", [P, T])
        phis = sb("phis", [P, T])
        mu_sb = sb("mu_sb", [P, NX, T])
        halfblk = sb("halfblk", [P, B, P])
        mbd = sb("mbd", [P, C, PH, C])
        eps = sb("eps", [P, 4])
        lg = sb("lg", [P, 8 * NX])
        tiny = sb("tiny", [P, 32])
        rw = sb("rw", [P, P])
        arm = sb("arm", [P, T])
        ars = sb("ars", [P, T])
        amax = sb("amax", [P, 4])
        gmax = sb("gmax", [P, 4])
        maskc = sb("maskc", [P, T])
        gh = sb("gh", [P, T4, PH, C], F16)
        gl = sb("gl", [P, T4, PH, C], F16)
        g01 = sb("g01", [P, T])
        st = sb("st", [P, 8])
        h = sb("h", [P, T])
        hsq = sb("hsq", [P, T])
        sqj = sb("sqj", [P, B, T])
        thr = sb("thr", [P, 2, B])
        hgraph = sb("hgraph", [P, B, 2, T])
        deg = sb("deg", [P, 2, B])
        rdeg = sb("rdeg", [P, 2, B])
        rdegb = sb("rdegb", [P, 2, B, C])
        rdegc = sb("rdegc", [P, T])
        xe = sb("xe", [P, 2, P])
        edgec = sb("edgec", [P, T])
        edget = sb("edget", [P, 2, B, C])
        conv = sb("conv", [P, T])
        bnst = sb("bnst", [P, B, 6])
        y = sb("y", [P, T])
        th = sb("th", [P, T])
        x1 = sb("x1", [P, T])
        xm = sb("xm", [P, T])
        sq = sb("sq", [P, T])
        std = sb("std", [P, 8])
        rstd = sb("rstd", [P, 8])
        rstdb = sb("rstdb", [P, 2, B, C])
        z = sb("z", [P, T])
        zt = sb("zt", [P, 2, B, C])
        e_sb = sb("e_sb", [P, B, 2, T])
        den = sb("den", [P, B, 2])
        o_sb = sb("o_sb", [P, T])
        t2 = sb("t2", [P, T])
        u32 = sb("u32", [P, T])
        u2 = sb("u2", [P, 2, B, T4], F16)
        yb = sb("yb", [P, T])
        res = sb("res", [P, T])

        ident = cst[:, IDENT:IDENT + P]
        logits, expl, soft, onehot, wts = (lg[:, n * NX:(n + 1) * NX] for n in range(5))
        lmax, lsum, smax, ws, sig, sc, isc, p2, wsel = (tiny[:, n:n + 1] for n in range(9))
        lrec, bnd, fmax = tiny[:, 9:10], tiny[:, 10:11], tiny[:, 11:12]
        ltmp = lg[:, 5 * NX:6 * NX]
        mean, var, gstd, grstd = (st[:, n:n + 1] for n in range(4))
        bnaff = sb("bnaff", [P, 8])
        bstd, brstd, ba, bb = (bnaff[:, n + 2:n + 3] for n in range(4))
        rs6 = sb("rs6", [P, 6])
        cs6 = sb("cs6", [P, 6])

        block = ctx.enter_context(nc.Block())

        def spots(name):
            names = list(SPOTS)
            a = sum(SPOTS[n] for n in names[:names.index(name)])
            return range(a, a + SPOTS[name])

        assert sum(SPOTS.values()) == NPAIR

        @block.sync
        def _(sp):
            sp.dma_start(x_sb[:, :], x).then_inc(sem("x_in"), 16)
            sp.dma_start(sml[:, :], small).then_inc(sem("small_in"), 16)
            sp.dma_start(phi_sb[:, :], phi4).then_inc(sem("phi_in"), 16)
            sp.dma_start(mu_sb[:, :, :], mu4.rearrange("p (i f) -> p i f", i=NX)).then_inc(sem("mu_in"), 16)
            sp.wait_ge(sem("res"), 1)
            sp.dma_start(out, res[:, :]).then_inc(sem("out"), 16)
            sp.wait_ge(sem("out"), 16)

        @block.gpsimd
        def _(pool):
            pool.memset(halfblk[:, :, :], 0.0).then_inc(sem("zero"), 1)
            pool.memset(mbd[:, :, :, :], 0.0).then_inc(sem("zero"), 1)
            pool.wait_ge(sem("zero"), 2)
            for b in range(B):
                pool.memset(halfblk[32 * b:32 * b + 32, b, :], 0.5).then_inc(sem("halfblk"), 1)
            pool.wait_ge(sem("phi_in"), 16)
            pool.wait_ge(sem("const_in"), 16)
            pool.wait_ge(sem("halfblk"), B)
            pool.tensor_tensor(phis[:, :], phi_sb[:, :], cst[:, SIGN:SIGN + T], ALU.mult).then_inc(sem("phis"), 1)
            pool.wait_ge(sem("amax"), 4)
            pool.partition_all_reduce(gmax[:, :], amax[:, :], P, RMAX).then_inc(sem("gmax"), 1)
            pool.wait_ge(sem("ars"), 1)
            pool.wait_ge(sem("g_low"), NPAIR)
            ghv = gh[:, 0:2, :, :].rearrange("p m r e -> p (m r e)")
            glv = gl[:, 0:2, :, :].rearrange("p m r e -> p (m r e)")
            pool.tensor_tensor(g01[:, :], ghv, glv, ALU.add).then_inc(sem("g01"), 1)
            pool.wait_ge(sem("g01"), 1)
            pool.tensor_tensor(g01[:, :], g01[:, :], ars[:, :], ALU.add).then_inc(sem("g01"), 1)
            pool.wait_ge(sem("g01"), 2)
            pool.tensor_copy(ghv, g01[:, :]).then_inc(sem("g01"), 1)
            pool.wait_ge(sem("g01"), 3)
            pool.tensor_tensor(glv, g01[:, :], ghv, ALU.subtract).then_inc(sem("g_ready"), 1)

        @block.scalar
        def _(act):
            act.dma_start(cst[:, :], consts).then_inc(sem("const_in"), 16)
            act.dma_start(m_sb[:, :], mfilt).then_inc(sem("m_in"), 16)

            def g_high(name):
                for q in spots(name):
                    act.wait_ge(sem("g_psum"), q + 1)
                    act.wait_ge(sem("scale"), 1)
                    act.activation(gh[:, :, :, 2 * q:2 * q + 2].rearrange("p m r e -> p e (m r)"),
                                   gbank[q % 2][:, :].rearrange("p (e f) -> p e f", e=2), ACT.Copy, scale=sc)\
                       .then_inc(sem("g_high"), 1)

            act.wait_ge(sem("eps"), 1)
            act.wait_ge(sem("gn_mv"), 1)
            act.activation(gstd, var, ACT.Sqrt, bias=eps[:, 0:1]).then_inc(sem("gn_std"), 1)
            act.wait_ge(sem("small_in"), 16)
            act.activation(sig, sml[:, P_SIGMA:P_SIGMA + 1], ACT.Sqrt).then_inc(sem("sig"), 1)
            act.wait_ge(sem("sig"), 1)
            act.activation(sig, sig, ACT.Sqrt).then_inc(sem("sig"), 1)
            act.wait_ge(sem("logits"), 1)
            act.activation(expl, ltmp, ACT.Exp).then_inc(sem("expl"), 1)
            act.wait_ge(sem("h"), 1)
            act.activation(hsq[:, :], h[:, :], ACT.Square).then_inc(sem("hsq"), 1)
            for n, bk in enumerate((chainA, chainB)):
                act.wait_ge(sem("sqj_psum"), n + 1)
                act.activation(sqj[:, 2 * n:2 * n + 2, :], bk[:, :].rearrange("p (b t) -> p b t", b=2), ACT.Copy)\
                   .then_inc(sem("sqj"), 1)
            act.wait_ge(sem("zero"), 2)
            act.wait_ge(sem("mix_psum"), 2)
            act.wait_ge(sem("amax"), 4)
            for j in range(PH):
                act.activation(mbd[32 * j:32 * j + 32, 16:32, j, :],
                               gbank[1][32 * j:32 * j + 32, :].rearrange("p (e d) -> p e d", d=C), ACT.Copy)\
                   .then_inc(sem("mbd_a"), 1)
            g_high("gram")
            g_high("compare")
            g_high("edge")
            act.wait_ge(sem("edge_psum"), 1)
            act.activation(edgec[:, :], chainA[:, 0:T], ACT.Copy).then_inc(sem("edgec"), 1)
            act.wait_ge(sem("rdeg"), 1)
            act.activation(rdegb[:, :, :, :], rdeg[:, :, :].unsqueeze(3).broadcast_to([P, 2, B, C]), ACT.Copy)\
               .then_inc(sem("rdegb"), 1)
            act.wait_ge(sem("rdegc_psum"), 1)
            act.activation(rdegc[:, :], chainA[:, 0:T], ACT.Copy).then_inc(sem("rdegc"), 1)
            g_high("vert")
            g_high("bn")
            act.wait_ge(sem("bn_mv"), 1)
            act.activation(bstd, bnaff[:, 1:2], ACT.Sqrt, bias=eps[:, 1:2]).then_inc(sem("bn_std"), 1)
            g_high("silu")
            act.wait_ge(sem("y"), 1)
            act.activation(th[:, :], y[:, :], ACT.Tanh, scale=0.5).then_inc(sem("th"), 1)
            g_high("ln1")
            act.wait_ge(sem("xm_psum"), 1)
            act.activation(sq[:, :], quad[:, 0, 0:T], ACT.Square).then_inc(sem("sq"), 1)
            act.wait_ge(sem("var_psum"), 1)
            act.activation(std[:, :], chainB[:, 0:8], ACT.Sqrt, bias=eps[:, 2:3]).then_inc(sem("std"), 1)
            g_high("scores")
            act.wait_ge(sem("zt_psum"), 1)
            act.activation(zt[:, :, :, :].rearrange("p h b c -> p (h b c)"), chainB[:, 0:T], ACT.Copy)\
               .then_inc(sem("zt"), 1)
            for b in range(B):
                act.wait_ge(sem("scores"), b + 1)
                act.activation(e_sb[:, b, :, :].rearrange("p h t -> p (h t)"), quad[:, b, :], ACT.Exp)\
                   .then_inc(sem("exp"), 1)
            g_high("av")
            act.wait_ge(sem("av"), 1)
            act.activation(o_sb[:, :], chainA[:, 0:T], ACT.Copy).then_inc(sem("o"), 1)
            g_high("ln2")
            act.wait_ge(sem("xm_psum"), 2)
            act.activation(sq[:, :].rearrange("p (b t) -> p b t", b=B), quad[:, :, 0:T4], ACT.Square)\
               .then_inc(sem("sq"), 1)
            act.wait_ge(sem("var_psum"), 2)
            act.activation(std[:, :], chainB[:, 0:8], ACT.Sqrt, bias=eps[:, 3:4], scale=USCALE ** -2)\
               .then_inc(sem("std"), 1)
            act.wait_ge(sem("u32"), 1)
            act.activation(u2[:, 0, :, :].rearrange("p b t -> p (b t)"), u32[:, :], ACT.Copy).then_inc(sem("u_high"), 1)

        @block.tensor
        def _(pe):
            def g_psum(name):
                for q in spots(name):
                    if q == 0:
                        pe.wait_ge(sem("phis"), 1)
                        pe.wait_ge(sem("mbd_a"), PH)
                        pe.wait_ge(sem("mbd_v"), PH)
                    if q >= 2:
                        pe.wait_ge(sem("g_low"), q - 1)
                    for n in range(2):
                        mm = pe.matmul(gbank[q % 2][:, n * T:(n + 1) * T],
                                       mbd[:, 2 * q + n, :, :].rearrange("p j d -> p (j d)"), phis[:, :],
                                       start=True, stop=True)
                    mm.then_inc(sem("g_psum"), 1)

            def turn(dst, src, signal):
                for n in range(2):
                    mm = pe.transpose(dst[:, n * P:(n + 1) * P], src[:, n * P:(n + 1) * P], ident)
                mm.then_inc(sem(signal), 1)

            pe.wait_ge(sem("m_in"), 16)
            pe.wait_ge(sem("rw"), 1)
            for n in range(2):
                pe.matmul(gbank[n][:, :], rw[:, :], m_sb[:, 512 * n:512 * n + 512], start=True, stop=True)\
                  .then_inc(sem("mix_psum"), 1)
            pe.wait_ge(sem("hsq"), 1)
            pe.wait_ge(sem("halfblk"), B)
            for b in range(B):
                mm = pe.matmul((chainA, chainB)[b // 2][:, (b % 2) * T:(b % 2) * T + T], halfblk[:, b, :], hsq[:, :],
                               start=True, stop=True)
                if b % 2:
                    mm.then_inc(sem("sqj_psum"), 1)
            for n in range(2):
                for b in range(B):
                    r = slice(32 * b, 32 * b + 32)
                    mm = pe.matmul(quad[:, b, n * T:(n + 1) * T], h[r, n * HT:(n + 1) * HT], h[r, :],
                                   start=True, stop=True)
                    mm.then_inc(sem("gram"), 1)
            pe.wait_ge(sem("sqj"), 1)
            for n in range(2):
                mm = pe.matmul(chainA[:, n * B:(n + 1) * B], hsq[:, n * HT:(n + 1) * HT], cst[:, COLHALF:COLHALF + B],
                               start=True, stop=True)
            mm.then_inc(sem("sqi_psum"), 1)
            pe.wait_ge(sem("sqj"), 2)
            for n in range(2):
                mm = pe.matmul(chainB[:, n * P:(n + 1) * P], h[:, n * HT:(n + 1) * HT], sml[:, P_WT:P_WT + P],
                               start=True, stop=True)
            mm.then_inc(sem("xe_psum"), 1)
            g_psum("gram")
            g_psum("compare")
            pe.wait_ge(sem("xe"), 1)
            pe.wait_ge(sem("thr"), 1)
            for b in range(B):
                for n in range(2):
                    if n == 0:
                        pe.wait_ge(sem("compare"), 2 * b + 2)
                    mm = pe.matmul(chainA[32 * b:32 * b + 32, 0:T], xe[:, n, 32 * b:32 * b + 32], hgraph[:, b, n, :],
                                   start=(n == 0), stop=(n == 1))
            mm.then_inc(sem("edge_psum"), 1)
            g_psum("edge")
            pe.wait_ge(sem("edgec"), 1)
            turn(chainB, edgec, "edget_psum")
            pe.wait_ge(sem("rdegb"), 1)
            turn(chainA, rdegb[:, :, :, :].rearrange("p h b c -> p (h b c)"), "rdegc_psum")
            g_psum("vert")
            pe.wait_ge(sem("edget"), 1)
            for n in range(2):
                for b in range(B):
                    mm = pe.matmul(quad[32 * b:32 * b + 32, 0, 0:T], edget[:, n, b, :], hgraph[:, b, n, :],
                                   start=(n == 0), stop=(n == 1))
            mm.then_inc(sem("vert_psum"), 1)
            g_psum("bn")
            pe.wait_ge(sem("bnst"), 1)
            pe.matmul(chainB[:, 0:B * 6], cst[:, SAME_C:SAME_C + P], bnst[:, :, :].rearrange("p b s -> p (b s)"),
                      start=True, stop=True).then_inc(sem("bn_psum"), 1)
            g_psum("silu")
            pe.wait_ge(sem("x1"), 1)
            pe.matmul(quad[:, 0, 0:T], cst[:, CENTER_BD:CENTER_BD + P], x1[:, :], start=True, stop=True)\
              .then_inc(sem("xm_psum"), 1)
            g_psum("ln1")

            def variance(n_th):
                pe.wait_ge(sem("sq"), n_th)
                for n in range(2):
                    mm = pe.matmul(chainB[:, n * B:(n + 1) * B], sq[:, n * P:(n + 1) * P], cst[:, COL32:COL32 + B],
                                   start=True, stop=True)
                mm.then_inc(sem("var_psum"), 1)
                pe.wait_ge(sem("rstdb"), n_th)
                turn(chainA, rstdb[:, :, :, :].rearrange("p h b c -> p (h b c)"), "rstdc_psum")

            variance(1)
            g_psum("scores")
            pe.wait_ge(sem("z"), 1)
            for b in range(B):
                r = slice(32 * b, 32 * b + 32)
                for n in range(2):
                    mm = pe.matmul(quad[:, b, n * T:(n + 1) * T], z[r, n * HT:(n + 1) * HT], z[r, :],
                                   start=True, stop=True)
                mm.then_inc(sem("scores"), 1)
                if b == 0:
                    turn(chainB, z, "zt_psum")
            g_psum("av")
            pe.wait_ge(sem("zt"), 1)
            for b in range(B):
                pe.wait_ge(sem("exp"), b + 1)
                for n in range(2):
                    mm = pe.matmul(chainA[32 * b:32 * b + 32, 0:T], zt[:, n, b, :], e_sb[:, b, n, :],
                                   start=(n == 0), stop=(n == 1))
            mm.then_inc(sem("av"), 1)
            pe.wait_ge(sem("rstdb"), 2)
            turn(chainB, rstdb[:, :, :, :].rearrange("p h b c -> p (h b c)"), "rden_psum")
            g_psum("ln2")
            pe.wait_ge(sem("t2"), 1)
            for j in range(PH):
                for b in range(B):
                    r = slice(32 * b, 32 * b + 32)
                    mm = pe.matmul(quad[32 * j:32 * j + 32, b, 0:T4],
                                   cst[r, CENTER_ALL + 32 * j:CENTER_ALL + 32 * j + 32], t2[r, j:T:PH],
                                   start=True, stop=True)
            mm.then_inc(sem("xm_psum"), 1)
            pe.wait_ge(sem("sq"), 2)
            for n in range(2):
                mm = pe.matmul(chainB[:, n * B:(n + 1) * B], sq[:, n * P:(n + 1) * P], cst[:, COL32:COL32 + B],
                               start=True, stop=True)
            mm.then_inc(sem("var_psum"), 1)
            pe.wait_ge(sem("rstdb"), 3)
            turn(chainA, rstdb[:, :, :, :].rearrange("p h b c -> p (h b c)"), "rstdc_psum")
            pe.wait_ge(sem("u_high"), 1)
            pe.wait_ge(sem("u_low"), 1)
            pe.wait_ge(sem("g_ready"), 1)
            acc = gbank[0][:, :].rearrange("p (s b t) -> p s b t", s=2, b=B)
            for m in range(T4):
                w = T4 - m
                pe.matmul(acc[:, :, :, m:T4], gh[:, m, :, :].rearrange("p r e -> p (r e)"), u2[:, :, :, 0:w],
                          start=(m == 0), stop=False, skip_group_check=True)
                mm = pe.matmul(acc[:, 0, :, m:T4], gl[:, m, :, :].rearrange("p r e -> p (r e)"), u2[:, 0, :, 0:w],
                               start=False, stop=(m == T4 - 1), skip_group_check=True)
            mm.then_inc(sem("stu_psum"), 1)
            pe.wait_ge(sem("stu"), 1)
            yv = yb[:, :].rearrange("p (b t) -> p b t", b=B)
            for b in range(B):
                for r in range(PH):
                    q = slice(32 * r, 32 * r + 32)
                    mm = pe.matmul(quad[32 * b:32 * b + 32, r, 0:T4], cst[q, IDENT + 32 * r:IDENT + 32 * r + 32],
                                   yv[q, b, :], start=True, stop=True)
            mm.then_inc(sem("back"), 1)

        @block.vector
        def _(dve):
            step = [0]

            def link(ins):
                step[0] += 1
                ins.then_inc(sem("dve_step"), 1)
                dve.wait_ge(sem("dve_step"), step[0])

            def g_low(name):
                for q in spots(name):
                    dve.wait_ge(sem("g_high"), q + 1)
                    dve.scalar_tensor_tensor(out=gl[:, :, :, 2 * q:2 * q + 2].rearrange("p m r e -> p (m r) e"),
                                             in0=gbank[q % 2][:, :].rearrange("p (e f) -> p f e", e=2), scalar=sc,
                                             in1=gh[:, :, :, 2 * q:2 * q + 2].rearrange("p m r e -> p (m r) e"),
                                             op0=ALU.mult, op1=ALU.subtract).then_inc(sem("g_low"), 1)

            for n, v in enumerate((GN_EPS, BN_EPS, LN_EPS, LN_EPS * USCALE ** -2)):
                ins = dve.memset(eps[:, n:n + 1], v)
            ins.then_inc(sem("eps"), 1)
            dve.wait_ge(sem("x_in"), 16)
            link(dve.bn_stats(rs6[:, :], x_sb[:, :]))
            dve.bn_aggr(st[:, 0:2], rs6[:, :]).then_inc(sem("gn_mv"), 1)
            dve.wait_ge(sem("gn_std"), 1)
            link(dve.reciprocal(grstd, gstd))
            dve.tensor_scalar(h[:, :], x_sb[:, :], mean, grstd, ALU.subtract, ALU.mult).then_inc(sem("h"), 1)
            dve.wait_ge(sem("small_in"), 16)
            link(dve.tensor_tensor(logits, sml[:, P_LOGW:P_LOGW + NX], sml[:, P_GUMBEL:P_GUMBEL + NX], ALU.add))
            link(dve.reduce_max(lmax, logits, AX_X))
            dve.tensor_scalar(ltmp, logits, lmax, None, ALU.subtract).then_inc(sem("logits"), 1)
            dve.wait_ge(sem("expl"), 1)
            link(dve.reduce_sum(lsum, expl, AX_X))
            link(dve.reciprocal(lrec, lsum))
            link(dve.tensor_scalar(soft, expl, lrec, None, ALU.mult))
            link(dve.reduce_max(smax, soft, AX_X))
            dve.wait_ge(sem("const_in"), 16)
            link(dve.scalar_tensor_tensor(out=ltmp, in0=soft, scalar=smax, in1=cst[:, FIRST:FIRST + NX],
                                          op0=ALU.is_equal, op1=ALU.mult))
            link(dve.reduce_max(fmax, ltmp, AX_X))
            link(dve.tensor_scalar(onehot, ltmp, fmax, None, ALU.is_equal))
            link(dve.tensor_tensor(wts, onehot, soft, ALU.subtract))
            link(dve.tensor_tensor(wts, wts, soft, ALU.add))
            link(dve.tensor_tensor_reduce(ltmp, wts, cst[:, EXPERT:EXPERT + NX], 1.0, 0.0, ALU.mult, ALU.add, wsel))
            dve.wait_ge(sem("sig"), 2)
            link(dve.tensor_tensor(ws, wsel, sig, ALU.mult))
            dve.tensor_scalar(rw[:, :], cst[:, REP_K:REP_K + P], ws, None, ALU.mult).then_inc(sem("rw"), 1)
            dve.wait_ge(sem("mu_in"), 16)
            link(dve.tensor_scalar(arm[:, :], mu_sb[:, 0, :], wts[:, 0:1], None, ALU.mult))
            for i in range(1, NX):
                link(dve.scalar_tensor_tensor(out=arm[:, :], in0=mu_sb[:, i, :], scalar=wts[:, i:i + 1], in1=arm[:, :],
                                              op0=ALU.mult, op1=ALU.add))
            dve.tensor_reduce(amax[:, 0:1], arm[:, :], AX_X, ALU.max, apply_absolute_value=True).then_inc(sem("amax"), 1)
            dve.wait_ge(sem("phi_in"), 16)
            dve.tensor_reduce(amax[:, 1:2], phi_sb[:, :], AX_X, ALU.max, apply_absolute_value=True)\
               .then_inc(sem("amax"), 1)
            for n in range(2):
                dve.wait_ge(sem("mix_psum"), n + 1)
                dve.tensor_reduce(amax[:, 2 + n:3 + n], gbank[n][:, :], AX_X, ALU.max, apply_absolute_value=True)\
                   .then_inc(sem("amax"), 1)
            dve.wait_ge(sem("zero"), 2)
            for j in range(PH):
                dve.tensor_copy(mbd[32 * j:32 * j + 32, 0:16, j, :],
                                gbank[0][32 * j:32 * j + 32, :].rearrange("p (e d) -> p e d", d=C))\
                   .then_inc(sem("mbd_v"), 1)
            dve.wait_ge(sem("gmax"), 1)
            link(dve.tensor_tensor(bnd, gmax[:, 2:3], gmax[:, 3:4], ALU.max))
            link(dve.scalar_tensor_tensor(out=bnd, in0=bnd, scalar=2.0 * K, in1=gmax[:, 1:2],
                                          op0=ALU.mult, op1=ALU.mult))
            link(dve.tensor_scalar(bnd, bnd, gmax[:, 0:1], 1e-30, ALU.add, ALU.max))
            link(dve.tensor_scalar(p2.bitcast(I32), bnd.bitcast(I32), 0x7F800000, None, ALU.bitwise_and))
            link(dve.reciprocal(isc, p2))
            link(dve.tensor_scalar(sc, isc, GTOP / 2, None, ALU.mult))
            dve.tensor_scalar(isc, p2, 2.0 / GTOP / USCALE, None, ALU.mult).then_inc(sem("scale"), 1)
            dve.tensor_scalar(ars[:, :], arm[:, :], sc, None, ALU.mult).then_inc(sem("ars"), 1)
            tm = cst[:, TMASK:TMASK + NX * T].rearrange("p (i t) -> p i t", i=NX)
            link(dve.tensor_scalar(maskc[:, :], tm[:, 0, :], onehot[:, 0:1], None, ALU.mult))
            for i in range(1, NX):
                link(dve.scalar_tensor_tensor(out=maskc[:, :], in0=tm[:, i, :], scalar=onehot[:, i:i + 1],
                                              in1=maskc[:, :], op0=ALU.mult, op1=ALU.add))
            dve.wait_ge(sem("scale"), 1)
            link(dve.tensor_scalar(maskc[:, :], maskc[:, :], isc, None, ALU.mult))

            dve.wait_ge(sem("sqi_psum"), 1)
            dve.tensor_scalar(thr[:, :, :].rearrange("p h b -> p (h b)"), chainA[:, 0:2 * B], -1.0, RADIUS2 / 2,
                              ALU.mult, ALU.add).then_inc(sem("thr"), 1)
            dve.wait_ge(sem("xe_psum"), 1)
            dve.tensor_tensor(xe[:, :, :], chainB[:, 0:2 * P].rearrange("p (h f) -> p h f", h=2),
                              sml[:, P_BIAS:P_BIAS + P].unsqueeze(1).broadcast_to([P, 2, P]), ALU.add)\
               .then_inc(sem("xe"), 1)
            g_low("gram")
            dve.wait_ge(sem("sqj"), 2)
            dve.wait_ge(sem("thr"), 1)
            dve.wait_ge(sem("gram"), 2 * B)
            for b in range(B):
                for n in range(2):
                    ins = dve.scalar_tensor_tensor(out=hgraph[:, b, n, :], in0=quad[:, b, n * T:(n + 1) * T],
                                                   scalar=thr[:, n, b:b + 1], in1=sqj[:, b, :],
                                                   op0=ALU.add, op1=ALU.is_gt, accum_out=deg[:, n, b:b + 1])
                    ins.then_inc(sem("compare"), 1)
            dve.wait_ge(sem("compare"), 2 * B)
            link(dve.tensor_scalar(deg[:, :, :], deg[:, :, :], 1.0, None, ALU.max))
            dve.reciprocal(rdeg[:, :, :], deg[:, :, :]).then_inc(sem("rdeg"), 1)
            g_low("compare")
            g_low("edge")
            dve.wait_ge(sem("rdeg"), 1)
            dve.wait_ge(sem("edget_psum"), 1)
            dve.tensor_tensor(edget[:, :, :, :], chainB[:, 0:T].rearrange("p (h b c) -> p h b c", h=2, b=B),
                              rdeg[:, :, :].unsqueeze(3).broadcast_to([P, 2, B, C]), ALU.mult)\
               .then_inc(sem("edget"), 1)
            g_low("vert")
            dve.wait_ge(sem("vert_psum"), 1)
            dve.wait_ge(sem("rdegc"), 1)
            link(dve.tensor_tensor(conv[:, :], quad[:, 0, 0:T], rdegc[:, :], ALU.mult))
            link(dve.tensor_tensor(conv[:, :], conv[:, :], h[:, :], ALU.add))
            link(dve.bn_stats(cs6[:, :], conv[:, :]))
            dve.tensor_tensor(bnst[:, :, :], cst[:, BMASK:BMASK + B * 6].rearrange("p (b s) -> p b s", b=B),
                              cs6[:, :].unsqueeze(1).broadcast_to([P, B, 6]), ALU.mult).then_inc(sem("bnst"), 1)
            g_low("bn")
            dve.wait_ge(sem("bn_psum"), 1)
            dve.bn_aggr(bnaff[:, 0:2], chainB[:, 0:B * 6]).then_inc(sem("bn_mv"), 1)
            dve.wait_ge(sem("bn_std"), 1)
            link(dve.reciprocal(brstd, bstd))
            link(dve.tensor_tensor(ba, brstd, sml[:, P_GAMMA:P_GAMMA + 1], ALU.mult))
            link(dve.scalar_tensor_tensor(out=bb, in0=ba, scalar=bnaff[:, 0:1], in1=sml[:, P_BETA:P_BETA + 1],
                                          op0=ALU.mult, op1=ALU.subtract))
            dve.tensor_scalar(y[:, :], conv[:, :], ba, bb, ALU.mult, ALU.subtract).then_inc(sem("y"), 1)
            g_low("silu")
            dve.wait_ge(sem("y"), 1)
            dve.wait_ge(sem("th"), 1)
            link(dve.scalar_tensor_tensor(out=th[:, :], in0=th[:, :], scalar=1.0, in1=y[:, :],
                                          op0=ALU.add, op1=ALU.mult))
            dve.scalar_tensor_tensor(out=x1[:, :], in0=th[:, :], scalar=0.5, in1=x_sb[:, :],
                                     op0=ALU.mult, op1=ALU.add).then_inc(sem("x1"), 1)
            g_low("ln1")

            def spread(n_th):
                dve.wait_ge(sem("std"), n_th)
                link(dve.reciprocal(rstd[:, :], std[:, :]))
                dve.tensor_copy(rstdb[:, :, :, :],
                                rstd[:, :].rearrange("p (h b) -> p h b", h=2).unsqueeze(3).broadcast_to([P, 2, B, C]))\
                   .then_inc(sem("rstdb"), 1)

            dve.wait_ge(sem("sq"), 1)
            dve.tensor_copy(xm[:, :], quad[:, 0, 0:T]).then_inc(sem("xm"), 1)
            spread(1)
            dve.wait_ge(sem("xm"), 1)
            dve.wait_ge(sem("rstdc_psum"), 1)
            dve.tensor_tensor(z[:, :], xm[:, :], chainA[:, 0:T], ALU.mult).then_inc(sem("z"), 1)
            g_low("scores")
            for b in range(B):
                dve.wait_ge(sem("exp"), b + 1)
                dve.reduce_sum(den[:, b, :], e_sb[:, b, :, :], AX_X).then_inc(sem("den"), 1)
            dve.wait_ge(sem("den"), B)
            link(dve.reciprocal(rstd[:, :].rearrange("p (b h) -> p b h", b=B), den[:, :, :]))
            dve.tensor_copy(rstdb[:, :, :, :],
                            rstd[:, :].rearrange("p (b h) -> p h b", b=B).unsqueeze(3).broadcast_to([P, 2, B, C]))\
               .then_inc(sem("rstdb"), 1)
            g_low("av")
            dve.wait_ge(sem("o"), 1)
            dve.wait_ge(sem("rden_psum"), 1)
            link(dve.tensor_tensor(t2[:, :], chainB[:, 0:T], o_sb[:, :], ALU.mult))
            dve.tensor_tensor(t2[:, :], t2[:, :], x1[:, :], ALU.add).then_inc(sem("t2"), 1)
            g_low("ln2")
            dve.wait_ge(sem("sq"), 2)
            dve.tensor_copy(xm[:, :].rearrange("p (b t) -> p b t", b=B), quad[:, :, 0:T4]).then_inc(sem("xm"), 1)
            spread(2)
            dve.wait_ge(sem("xm"), 2)
            dve.wait_ge(sem("rstdc_psum"), 2)
            dve.tensor_tensor(u32[:, :], xm[:, :], chainA[:, 0:T], ALU.mult).then_inc(sem("u32"), 1)
            dve.wait_ge(sem("u32"), 1)
            dve.wait_ge(sem("u_high"), 1)
            dve.tensor_tensor(u2[:, 1, :, :].rearrange("p b t -> p (b t)"), u32[:, :],
                              u2[:, 0, :, :].rearrange("p b t -> p (b t)"), ALU.subtract).then_inc(sem("u_low"), 1)
            dve.wait_ge(sem("stu_psum"), 1)
            link(dve.tensor_copy(yb[:, :], gbank[0][:, T:2 * T]))
            dve.tensor_tensor(yb[:, :], gbank[0][:, 0:T], yb[:, :], ALU.add).then_inc(sem("stu"), 1)
            dve.wait_ge(sem("back"), 1)
            rv = res[:, :].rearrange("p (t r) -> p r t", r=PH)
            link(dve.tensor_tensor(rv, quad[:, :, 0:T4], maskc[:, :].rearrange("p (t r) -> p r t", r=PH), ALU.mult))
            dve.tensor_tensor(res[:, :], res[:, :], t2[:, :], ALU.add).then_inc(sem("res"), 1)


def constants():
    p = np.arange(P)
    group, chan = p // C, p % C
    same_group = group[:, None] == group[None, :]
    same_chan = chan[:, None] == chan[None, :]
    center = same_chan - 1.0 / C
    k = p % K
    minus = (p // K) % 2
    j = p // (2 * K)
    f = np.arange(T)
    tau = f[None, :] - j[:, None]
    sign = np.where((minus[:, None] == 1) & (tau % 2 == 1), -1.0, 1.0)
    c = np.zeros((P, NCONST))
    c[:, IDENT:IDENT + P] = np.eye(P)
    c[:, CENTER_BD:CENTER_BD + P] = center * same_group
    c[:, CENTER_ALL:CENTER_ALL + P] = center
    c[:, SAME_C:SAME_C + P] = same_chan
    c[:, REP_K:REP_K + P] = (k[:, None] == k[None, :]) & (minus[:, None] == minus[None, :])
    c[:, SIGN:SIGN + T] = sign
    c[:, COL32:COL32 + B] = (group[:, None] == np.arange(B)) / C
    c[:, COLHALF:COLHALF + B] = (group[:, None] == np.arange(B)) / 2
    c[:, EXPERT:EXPERT + NX] = group[:, None] == np.arange(NX)
    c[:, BMASK:BMASK + B * 6] = np.repeat(group[:, None] == np.arange(B), 6, axis=1)
    for i in range(NX):
        c[:, TMASK + i * T:TMASK + (i + 1) * T] = f < T >> i
    c[:, FIRST:FIRST + NX] = np.arange(NX, 0, -1)
    return c.astype(np.float32)


def kernel(x, L0_conv_W_fc, L0_conv_b_fc, L0_conv_gamma, L0_conv_beta, L1_ffn_sigma, L1_ffn_phi, L1_ffn_M_u,
           L1_ffn_M_phi_plus, L1_ffn_M_phi_minus, L1_ffn_log_weights, L1_ffn_gumbel):
    import concourse.bacc as bacc
    from concourse.bass_utils import run_bass_kernel_spmd

    as_np = np.asarray
    small = np.zeros((P, NSMALL), np.float32)
    for b in range(B):
        small[32 * b:32 * b + 32, P_WT + 32 * b:P_WT + 32 * b + 32] = as_np(L0_conv_W_fc).T
    small[:, P_BIAS:P_BIAS + P] = np.tile(as_np(L0_conv_b_fc), B)
    small[:, P_GAMMA] = np.tile(as_np(L0_conv_gamma), B)
    small[:, P_BETA] = np.tile(as_np(L0_conv_beta), B)
    small[:, P_SIGMA] = np.tile(as_np(L1_ffn_sigma), P // K)
    small[:, P_LOGW:P_LOGW + NX] = as_np(L1_ffn_log_weights)
    small[:, P_GUMBEL:P_GUMBEL + NX] = as_np(L1_ffn_gumbel)
    mfilt = np.stack([as_np(L1_ffn_M_phi_plus), as_np(L1_ffn_M_phi_minus)], 1).transpose(0, 1, 2, 4, 3).reshape(P, C * C)
    phi = as_np(L1_ffn_phi)
    phi4 = np.zeros((PH, 2, K, T), np.float32)
    for j in range(PH):
        phi4[j, :, :, j:] = phi[:T - j].T
    mu = as_np(L1_ffn_M_u)
    mu4 = np.zeros((PH, C, NX, 2 * PH, C), np.float32)
    for j in range(PH):
        for tap in range(NTAU):
            mu4[j, :, :, j + tap, :] = mu[:, tap].transpose(1, 0, 2)

    ins = {
        "in_x": np.ascontiguousarray(as_np(x)).reshape(P, T),
        "in_consts": constants(),
        "in_small": small,
        "in_mfilt": np.ascontiguousarray(mfilt),
        "in_phi4": phi4.reshape(P, T),
        "in_mu4": mu4.reshape(P, NX * T),
    }
    nc = bacc.Bacc("TRN2", target_bir_lowering=False, num_devices=1)
    aps = [nc.dram_tensor(n, a.shape, mybir.dt.from_np(a.dtype), kind="ExternalInput").ap() for n, a in ins.items()]
    out = nc.dram_tensor("out", (P, T), F32, kind="ExternalOutput").ap()
    stu_hybrid_kernel(nc, *aps, out)
    r = run_bass_kernel_spmd(nc, [ins], core_ids=[0])
    return r.results[0]["out"].reshape(B, C, 16, 16)
```

```python
from contextlib import ExitStack

import numpy as np

import concourse.bass as bass
from concourse import mybir

ALU = mybir.AluOpType
ACT = mybir.ActivationFunctionType
F32 = mybir.dt.float32
F16 = mybir.dt.float16
I32 = mybir.dt.int32
AX_X = mybir.AxisListType.X
RMAX = bass.bass_isa.ReduceOp.max

B, C, T = 4, 32, 256
P = B * C
HT = T // 2
NX = 4
K = 16
NTAU = 3
PH = P // C
PA = P // C
NM = T // PH
NS = NM // PA
NG = 4
EG = C // NG
PAD = PH
BN_EPS = 1e-5
GN_EPS = 1e-5
LN_EPS = 1e-5
RADIUS2 = 16.0 ** 2
USCALE = 256.0
PTOP = 16.0
TINY = 1e-15

IDENT, CENTER, SAME_C, REP_K = (n * P for n in range(4))
SIGN = 4 * P
COL32 = SIGN + 2
BMASK = COL32 + B
NCONST = BMASK + B * 6
P_WT, P_BIAS, P_GAMMA, P_BETA, P_SIGMA, P_LOGW, P_GUMBEL = 0, P, 2 * P, 2 * P + 1, 2 * P + 2, 2 * P + 3, 2 * P + 7
P_EXPERT = P_GUMBEL + NX
P_RANK = P_EXPERT + NX
NSMALL = P_RANK + NX

SPOTS = dict(silu=1, ln1=1, z=1, scores=1)
WARM_START, WARM_LN2, WARM_VAR = 7, 2, 4


def stu_hybrid_kernel(nc, x, consts, small, mfilt, phi, mu, out):
    with ExitStack() as ctx:
        def sb(name, shape, dt=F32):
            return ctx.enter_context(nc.sbuf_tensor(name, shape, dt))

        sems = {}

        def sem(name):
            if name not in sems:
                sems[name] = ctx.enter_context(nc.semaphore("s_" + name))
            return sems[name]

        bank = [ctx.enter_context(nc.psum_tensor(f"bank{i}", [P, 512], F32)) for i in range(4)]
        quad = ctx.enter_context(nc.psum_tensor("quad", [P, 4, 512], F32))
        chainA, chainB, gbank = bank[0], bank[1], bank[2:4]

        x_sb = sb("x_sb", [P, T])
        cst = sb("cst", [P, NCONST])
        ident16 = sb("ident16", [P, P], F16)
        sml = sb("sml", [P, NSMALL])
        m_sb = sb("m_sb", [P, C * C])
        phi_sb = sb("phi_sb", [P, T])
        phis = sb("phis", [P, T])
        mu_sb = sb("mu_sb", [P, NX, C])
        mumix = sb("mumix", [P, C])
        mtap = sb("mtap", [P, C])
        halfblk = sb("halfblk", [P, B, P], F16)
        hq = sb("hq", [P, 2, T], F16)
        busy = sb("busy", [P, 512], F16)
        spare = sb("spare", [P, 8])
        cover = sb("cover", [P, NX])
        mask0 = sb("mask0", [P, T + PH * PA])
        maskp = sb("maskp", [P, T])
        eps = sb("eps", [P, 4])
        lg = sb("lg", [P, 6 * NX])
        tiny = sb("tiny", [P, 32])
        wsum = sb("wsum", [P, NX])
        rw = sb("rw", [P, P])
        amax = sb("amax", [P, 4])
        gmaxp = sb("gmaxp", [P, 1])
        gmaxm = sb("gmaxm", [P, 2])
        mst = sb("mst", [P, C, C], F16)
        phst = sb("phst", [P, T], F16)
        gh = sb("gh", [P, NM, C], F16)
        gl = sb("gl", [P, NM, C], F16)
        g0 = sb("g0", [P, C])
        st = sb("st", [P, 8])
        h = sb("h", [P, T])
        blk = sb("blk", [P, B, T])
        hsq = sb("hsq", [P, T])
        sqj = sb("sqj", [P, B, T])
        thr = sb("thr", [P, 2, B])
        hgraph = sb("hgraph", [P, B, 2, T])
        deg = sb("deg", [P, 2, B])
        rdeg = sb("rdeg", [P, 2, B])
        rdegb = sb("rdegb", [P, 2, B, C])
        rdegc = sb("rdegc", [P, T])
        xe = sb("xe", [P, 2, P])
        edgec = sb("edgec", [P, T])
        edget = sb("edget", [P, 2, B, C])
        conv = sb("conv", [P, T])
        bnst = sb("bnst", [P, B, 6])
        y = sb("y", [P, T])
        th = sb("th", [P, T])
        x1 = sb("x1", [P, T])
        xm = sb("xm", [P, T])
        sq = sb("sq", [P, T])
        std = sb("std", [P, 8])
        rstd = sb("rstd", [P, 8])
        rstdb = sb("rstdb", [P, 2, B, C])
        z = sb("z", [P, T])
        zt = sb("zt", [P, 2, B, C])
        e_sb = sb("e_sb", [P, B, 2, T])
        den = sb("den", [P, 2, B])
        o_sb = sb("o_sb", [P, T])
        t2 = sb("t2", [P, T])
        u32 = sb("u32", [P, T])
        u2 = sb("u2", [P, 2, PAD + T], F16)
        v2 = sb("v2", [P, 2, B, T], F16)
        yb = sb("yb", [P, B, T])
        res = sb("res", [P, T])

        ident = cst[:, IDENT:IDENT + P]
        logits, expl, soft, ranked, wts, onehot = (lg[:, n * NX:(n + 1) * NX] for n in range(6))
        lmax, lsum, smax, ws, sig, sc_m, isc, p2_m, sc_phi, p2_phi, lrec, bnd, fmax = \
            (tiny[:, n:n + 1] for n in range(13))
        mean, var, gstd, grstd = (st[:, n:n + 1] for n in range(4))
        bnaff = sb("bnaff", [P, 8])
        bstd, brstd, ba, bb, ba2, bb2 = (bnaff[:, n + 2:n + 3] for n in range(6))
        rs6 = sb("rs6", [P, 6])
        cs6 = sb("cs6", [P, 6])

        block = ctx.enter_context(nc.Block())

        def spots(name):
            names = list(SPOTS)
            a = sum(SPOTS[n] for n in names[:names.index(name)])
            return range(a, a + SPOTS[name])

        assert sum(SPOTS.values()) == NG

        @block.sync
        def _(sp):
            sp.dma_start(x_sb[:, :], x).then_inc(sem("x_in"), 16)
            sp.dma_start(phi_sb[:, :], phi).then_inc(sem("phi_in"), 16)
            sp.dma_start(m_sb[:, :], mfilt).then_inc(sem("m_in"), 16)
            sp.dma_start(cst[:, :], consts).then_inc(sem("const_in"), 16)
            sp.dma_start(mu_sb[:, :, :], mu.rearrange("p (i f) -> p i f", i=NX)).then_inc(sem("mu_in"), 16)
            sp.wait_ge(sem("res"), 1)
            sp.dma_start(out, res[:, :]).then_inc(sem("out"), 16)
            sp.wait_ge(sem("out"), 16)

        @block.gpsimd
        def _(pool):
            step = [0]

            def link(ins):
                step[0] += 1
                ins.then_inc(sem("pool_step"), 1)
                pool.wait_ge(sem("pool_step"), step[0])

            link(pool.memset(halfblk[:, :, :], 0.0))
            for b in range(B):
                pool.memset(halfblk[32 * b:32 * b + 32, b, :], 0.5).then_inc(sem("halfblk"), 1)
            pool.wait_ge(sem("halfblk"), B)
            pool.memset(blk[:, :, :], 0.0).then_inc(sem("zero"), 1)
            pool.memset(u2[:, :, 0:PAD], 0.0).then_inc(sem("zero"), 1)
            pool.wait_ge(sem("amax"), 1)
            pool.wait_ge(sem("zero"), 2)
            pool.partition_all_reduce(gmaxp[:, :], amax[:, 0:1], P, RMAX).then_inc(sem("gmaxp"), 1)
            pool.wait_ge(sem("const_in"), 16)
            pool.wait_ge(sem("scale_phi"), 1)
            pool.wait_ge(sem("gmaxp"), 1)
            link(pool.tensor_scalar(phis[:, :], phi_sb[:, :], sc_phi, 0.0, ALU.mult, ALU.add))
            link(pool.tensor_tensor(phis[:, :].rearrange("p (m s) -> p m s", s=2),
                                    phis[:, :].rearrange("p (m s) -> p m s", s=2),
                                    cst[:, SIGN:SIGN + 2].unsqueeze(1).broadcast_to([P, HT, 2]), ALU.mult))
            link(pool.tensor_scalar(phst[:, :], phis[:, :], 1.0, 0.0, ALU.mult, ALU.add))
            for g in (1, 3):
                r = slice(32 * g, 32 * g + 32)
                pool.tensor_tensor(phst[r, :], phis[r, :], phst[r, :], ALU.subtract).then_inc(sem("phst"), 1)
            pool.wait_ge(sem("mu_in"), 16)
            pool.wait_ge(sem("wts"), 1)
            pool.wait_ge(sem("phst"), 2)
            link(pool.tensor_tensor(mu_sb[:, :, :], mu_sb[:, :, :], wts.unsqueeze(2).broadcast_to([P, NX, C]),
                                    ALU.mult))
            link(pool.tensor_tensor(mu_sb[:, 0:2, :], mu_sb[:, 0:2, :], mu_sb[:, 2:4, :], ALU.add))
            pool.tensor_tensor(mumix[:, :], mu_sb[:, 0, :], mu_sb[:, 1, :], ALU.add).then_inc(sem("mumix"), 1)
            pool.wait_ge(sem("amax"), 3)
            pool.wait_ge(sem("mumix"), 1)
            pool.partition_all_reduce(gmaxm[:, :], amax[:, 1:3], P, RMAX).then_inc(sem("gmaxm"), 1)
            pool.wait_ge(sem("scale_m"), 1)
            pool.wait_ge(sem("gmaxm"), 1)
            link(pool.tensor_scalar(mtap[:, :], mumix[:, :], sc_m, 0.0, ALU.mult, ALU.add))
            link(pool.tensor_scalar(mtap[:, :], mtap[:, :], sc_phi, 0.0, ALU.mult, ALU.add))
            pool.wait_ge(sem("onehot"), 1)
            link(pool.tensor_scalar(cover[:, :], onehot, isc, 0.0, ALU.mult, ALU.add))
            for i in range(1, NX):
                link(pool.tensor_tensor(cover[:, i:i + 1], cover[:, i:i + 1], cover[:, i - 1:i], ALU.add))
            link(pool.memset(mask0[:, :], 0.0))
            for i in range(NX):
                lo = 0 if i == NX - 1 else T >> (i + 1)
                seg = mask0[:, lo:T >> i]
                pool.tensor_scalar(seg, seg, cover[:, i:i + 1], 0.0, ALU.add, ALU.add).then_inc(sem("mask"), 1)
            pool.wait_ge(sem("mask"), NX)
            for a in range(PA):
                r = slice(32 * a, 32 * a + 32)
                pool.tensor_scalar(maskp[r, :], mask0[r, PH * a:PH * a + T], 1.0, 0.0, ALU.mult, ALU.add)\
                    .then_inc(sem("mask"), 1)
            pool.wait_ge(sem("g_low"), NG)
            pool.wait_ge(sem("mask"), NX + PA)
            link(pool.tensor_tensor(g0[:, :], gh[:, 0, :], gl[:, 0, :], ALU.add))
            link(pool.tensor_tensor(g0[:, :], g0[:, :], mtap[:, :], ALU.add))
            link(pool.tensor_scalar(gh[:, 0, :], g0[:, :], 1.0, 0.0, ALU.mult, ALU.add))
            pool.tensor_tensor(gl[:, 0, :], g0[:, :], gh[:, 0, :], ALU.subtract).then_inc(sem("g_ready"), 1)

        @block.scalar
        def _(act):
            act.dma_start(sml[:, :], small).then_inc(sem("small_in"), 16)

            loads = []

            def tables(func):
                loads.append(func)
                act.activation(spare[:, len(loads) - 1:len(loads)], eps[:, 0:1], func)

            def g_high(name):
                for q in spots(name):
                    act.wait_ge(sem("g_psum"), q + 1)
                    act.activation(gh[:, :, EG * q:EG * q + EG].rearrange("p m e -> p e m"),
                                   gbank[q % 2][:, :].rearrange("p (e m) -> p e m", e=EG), ACT.Copy)\
                       .then_inc(sem("g_high"), 1)

            act.wait_ge(sem("eps"), 1)
            tables(ACT.Sqrt)
            act.wait_ge(sem("gn_mv"), 1)
            act.activation(gstd, var, ACT.Sqrt, bias=eps[:, 0:1]).then_inc(sem("gn_std"), 1)
            act.wait_ge(sem("small_in"), 16)
            act.activation(sig, sml[:, P_SIGMA:P_SIGMA + 1], ACT.Sqrt).then_inc(sem("sig"), 1)
            act.wait_ge(sem("sig"), 1)
            act.activation(sig, sig, ACT.Sqrt).then_inc(sem("sig"), 1)
            act.wait_ge(sem("h"), 1)
            act.activation(hq[:, 0, :], h[:, :], ACT.Square).then_inc(sem("hsq_high"), 1)
            act.wait_ge(sem("zero"), 1)
            for b in (2, 3):
                r = slice(32 * b, 32 * b + 32)
                act.activation(blk[r, b, :], h[r, :], ACT.Copy).then_inc(sem("blk_a"), 1)
            for n, bk in enumerate((chainA, chainB)):
                act.wait_ge(sem("sqj_psum"), n + 1)
                act.activation(sqj[:, 2 * n:2 * n + 2, :], bk[:, :].rearrange("p (b t) -> p b t", b=2), ACT.Copy)\
                   .then_inc(sem("sqj"), 1)
            act.wait_ge(sem("logits"), 1)
            act.activation(expl, ranked, ACT.Exp, accum_out=lsum).then_inc(sem("expl"), 1)
            tables(ACT.Sqrt)
            act.wait_ge(sem("const_in"), 16)
            act.activation(ident16[:, :], ident, ACT.Copy).then_inc(sem("ident16"), 1)
            act.wait_ge(sem("rdeg"), 1)
            act.activation(rdegb[:, :, :, :], rdeg[:, :, :].unsqueeze(3).broadcast_to([P, 2, B, C]), ACT.Copy)\
               .then_inc(sem("rdegb"), 1)
            act.wait_ge(sem("edge_psum"), 1)
            act.activation(edgec[:, :], chainA[:, 0:T], ACT.Copy).then_inc(sem("edgec"), 1)
            act.wait_ge(sem("rdegc_psum"), 1)
            act.activation(rdegc[:, :], chainA[:, 0:T], ACT.Copy).then_inc(sem("rdegc"), 1)
            act.wait_ge(sem("bn_mv"), 1)
            act.activation(bstd, bnaff[:, 1:2], ACT.Sqrt, bias=eps[:, 1:2]).then_inc(sem("bn_std"), 1)
            tables(ACT.Exp)
            act.wait_ge(sem("halves"), 1)
            act.activation(th[:, :], conv[:, :], ACT.Tanh, scale=ba2, bias=bb2).then_inc(sem("th"), 1)
            tables(ACT.Sqrt)
            for n in range(2):
                act.wait_ge(sem("mix_psum"), n + 1)
                act.activation(mst[:, 16 * n:16 * n + 16, :], gbank[n][:, :].rearrange("p (e d) -> p e d", d=C),
                               ACT.Copy).then_inc(sem("mst_high"), 1)
            act.wait_ge(sem("xm_psum"), 1)
            act.activation(sq[:, :], quad[:, 3, 0:T], ACT.Square).then_inc(sem("sq"), 1)
            g_high("silu")
            act.wait_ge(sem("var_psum"), 1)
            act.activation(std[:, :], chainB[:, 0:8], ACT.Sqrt, bias=eps[:, 2:3]).then_inc(sem("std"), 1)
            tables(ACT.Exp)
            g_high("ln1")
            for b in (2, 3):
                act.wait_ge(sem("z"), 1)
                r = slice(32 * b, 32 * b + 32)
                act.activation(blk[r, b, :], z[r, :], ACT.Copy).then_inc(sem("blk_a"), 1)
            g_high("z")
            act.wait_ge(sem("zt_psum"), 1)
            act.activation(zt[:, :, :, :].rearrange("p h b c -> p (h b c)"), chainB[:, 0:T], ACT.Copy)\
               .then_inc(sem("zt"), 1)
            for b in range(B):
                act.wait_ge(sem("scores"), b + 1)
                for n in range(2):
                    act.activation(e_sb[:, b, n, :], quad[:, b, n * T:(n + 1) * T], ACT.Exp,
                                   accum_out=den[:, n, b:b + 1]).then_inc(sem("exp"), 1)
            tables(ACT.Sqrt)
            act.wait_ge(sem("av"), 1)
            act.activation(o_sb[:, :], chainA[:, 0:T], ACT.Copy).then_inc(sem("o"), 1)
            g_high("scores")
            act.wait_ge(sem("xm_psum"), 2)
            act.activation(sq[:, :], quad[:, 3, 0:T], ACT.Square).then_inc(sem("sq"), 1)
            act.wait_ge(sem("var_psum"), 2)
            act.activation(std[:, :], chainB[:, 0:8], ACT.Sqrt, bias=eps[:, 3:4], scale=USCALE ** -2)\
               .then_inc(sem("std"), 1)
            for bk in range(3):
                act.wait_ge(sem("v_psum"), bk + 1)
                act.activation(v2[:, bk // 2, 2 * (bk % 2):2 * (bk % 2) + 2, :],
                               quad[:, bk, :].rearrange("p (b t) -> p b t", b=2), ACT.Copy).then_inc(sem("v"), 1)

        @block.tensor
        def _(pe):
            def g_psum(name):
                for n in spots(name):
                    if n == 0:
                        pe.wait_ge(sem("phst"), 2)
                        pe.wait_ge(sem("mst_low"), 2)
                    if n >= 2:
                        pe.wait_ge(sem("g_low"), n - 1)
                    for e in range(EG):
                        for q in range(PH):
                            mm = pe.matmul(gbank[n % 2][32 * q:32 * q + 32, NM * e:NM * e + NM],
                                           mst[:, EG * n + e, :], phst[:, q:T:PH], start=True, stop=True)
                    mm.then_inc(sem("g_psum"), 1)

            def keep_busy(dst, count):
                for _ in range(count):
                    pe.matmul(dst, busy[:, 0:P], busy[:, :], start=True, stop=True)

            def turn(dst, src, signal):
                for n in range(2):
                    mm = pe.transpose(dst[:, n * P:(n + 1) * P], src[:, n * P:(n + 1) * P], ident)
                mm.then_inc(sem(signal), 1)

            def gram(b, src, signal, nth):
                if b < 2:
                    pe.wait_ge(sem("blk_v"), 2 * nth + b + 1)
                else:
                    pe.wait_ge(sem("blk_a"), 2 * nth + b - 1)
                for n in range(2):
                    mm = pe.matmul(quad[:, b, n * T:(n + 1) * T], blk[:, b, n * HT:(n + 1) * HT], src[:, :],
                                   start=True, stop=True)
                mm.then_inc(sem(signal), 1)

            def mix(n):
                pe.matmul(gbank[n][:, :], rw[:, :], m_sb[:, 512 * n:512 * n + 512], start=True, stop=True)\
                  .then_inc(sem("mix_psum"), 1)

            def edge_sums(b):
                pe.wait_ge(sem("compare"), 2 * b + 2)
                for n in range(2):
                    mm = pe.matmul(chainA[32 * b:32 * b + 32, 0:T], xe[:, n, 32 * b:32 * b + 32], hgraph[:, b, n, :],
                                   start=(n == 0), stop=(n == 1))
                return mm

            pe.wait_ge(sem("busy"), 1)
            keep_busy(gbank[1][:, :], WARM_START)
            pe.wait_ge(sem("h"), 1)
            gram(0, h, "gram", 0)
            pe.wait_ge(sem("hsq_high"), 1)
            pe.wait_ge(sem("hsq_low"), 1)
            pe.wait_ge(sem("halfblk"), B)
            for b in range(B):
                for part in range(2):
                    mm = pe.matmul((chainA, chainB)[b // 2][:, (b % 2) * T:(b % 2) * T + T], halfblk[:, b, :],
                                   hq[:, part, :], start=(part == 0), stop=(part == 1))
                if b % 2:
                    mm.then_inc(sem("sqj_psum"), 1)
                if b == 1:
                    for n in range(2):
                        for part in range(2):
                            mm = pe.matmul(gbank[0][:, n * B:(n + 1) * B], hq[:, part, n * HT:(n + 1) * HT],
                                           halfblk[:, :, 0], start=(part == 0), stop=(part == 1))
                    mm.then_inc(sem("sqi_psum"), 1)
            gram(1, h, "gram", 0)
            pe.wait_ge(sem("small_in"), 16)
            for n in range(2):
                mm = pe.matmul(gbank[1][:, n * P:(n + 1) * P], h[:, n * HT:(n + 1) * HT], sml[:, P_WT:P_WT + P],
                               start=True, stop=True)
            mm.then_inc(sem("xe_psum"), 1)
            gram(2, h, "gram", 0)
            gram(3, h, "gram", 0)
            pe.wait_ge(sem("xe"), 1)
            pe.wait_ge(sem("sqj"), 1)
            for b in range(B):
                mm = edge_sums(b)
            mm.then_inc(sem("edge_psum"), 1)
            pe.wait_ge(sem("const_in"), 16)
            pe.wait_ge(sem("edgec"), 1)
            pe.wait_ge(sem("sqj"), 2)
            turn(chainB, edgec, "edget_psum")
            pe.wait_ge(sem("rdegb"), 1)
            turn(chainA, rdegb[:, :, :, :].rearrange("p h b c -> p (h b c)"), "rdegc_psum")
            pe.wait_ge(sem("edget"), 1)
            for n in range(2):
                for b in range(B):
                    mm = pe.matmul(quad[32 * b:32 * b + 32, 0, 0:T], edget[:, n, b, :], hgraph[:, b, n, :],
                                   start=(n == 0), stop=(n == 1))
            mm.then_inc(sem("vert_psum"), 1)
            pe.wait_ge(sem("bnst"), 1)
            pe.matmul(chainB[:, 0:B * 6], cst[:, SAME_C:SAME_C + P], bnst[:, :, :].rearrange("p b s -> p (b s)"),
                      start=True, stop=True).then_inc(sem("bn_psum"), 1)
            pe.wait_ge(sem("m_in"), 16)
            pe.wait_ge(sem("rw"), 1)
            pe.wait_ge(sem("thr"), 1)
            mix(0)
            mix(1)
            pe.wait_ge(sem("x1"), 1)
            pe.matmul(quad[:, 3, 0:T], cst[:, CENTER:CENTER + P], x1[:, :], start=True, stop=True)\
              .then_inc(sem("xm_psum"), 1)
            g_psum("silu")

            def variance(n_th):
                pe.wait_ge(sem("sq"), n_th)
                for n in range(2):
                    mm = pe.matmul(chainB[:, n * B:(n + 1) * B], sq[:, n * P:(n + 1) * P], cst[:, COL32:COL32 + B],
                                   start=True, stop=True)
                mm.then_inc(sem("var_psum"), 1)

            variance(1)
            g_psum("ln1")
            pe.wait_ge(sem("rstdb"), 1)
            turn(chainA, rstdb[:, :, :, :].rearrange("p h b c -> p (h b c)"), "rstdc_psum")
            g_psum("z")
            pe.wait_ge(sem("z"), 1)
            gram(0, z, "scores", 1)
            turn(chainB, z, "zt_psum")
            for b in range(1, B):
                gram(b, z, "scores", 1)
            g_psum("scores")
            pe.wait_ge(sem("zt"), 1)
            for b in range(B):
                pe.wait_ge(sem("exp"), 2 * b + 2)
                for n in range(2):
                    mm = pe.matmul(chainA[32 * b:32 * b + 32, 0:T], zt[:, n, b, :], e_sb[:, b, n, :],
                                   start=(n == 0), stop=(n == 1))
            mm.then_inc(sem("av"), 1)
            pe.wait_ge(sem("rstdb"), 2)
            turn(chainB, rstdb[:, :, :, :].rearrange("p h b c -> p (h b c)"), "rden_psum")
            pe.wait_ge(sem("t2"), 1)
            pe.matmul(quad[:, 3, 0:T], cst[:, CENTER:CENTER + P], t2[:, :], start=True, stop=True)\
              .then_inc(sem("xm_psum"), 1)
            pe.wait_ge(sem("g_low"), NG)
            keep_busy(gbank[1][:, :], WARM_LN2)
            variance(2)
            keep_busy(gbank[1][:, :], WARM_VAR)
            pe.wait_ge(sem("rstdb"), 3)
            turn(chainA, rstdb[:, :, :, :].rearrange("p h b c -> p (h b c)"), "rstdc_psum")
            pe.wait_ge(sem("std"), 2)
            pe.matmul(chainB[:, 0:T], ident, t2[:, :], start=True, stop=False, skip_group_check=True)
            pe.wait_ge(sem("ident16"), 1)
            pe.wait_ge(sem("zero"), 2)
            pe.wait_ge(sem("xm"), 2)
            for part, signal in enumerate(("u_high", "u_low")):
                pe.wait_ge(sem(signal), 1)
                for b in range(B):
                    for q in range(PH):
                        mm = pe.matmul(quad[32 * q:32 * q + 32, 2 * part + b // 2, (b % 2) * T:(b % 2) * T + T],
                                       ident16[:, 32 * b:32 * b + 32], u2[:, part, PAD - q:PAD - q + T],
                                       start=True, stop=True)
                    if b % 2:
                        mm.then_inc(sem("v_psum"), 1)
            pe.wait_ge(sem("g_ready"), 1)
            for pair in range(2):
                acc = gbank[pair][:, :].rearrange("p (b t) -> p b t", b=2)
                for g, part in ((gl, 0), (gh, 0), (gh, 1)):
                    if part == 0:
                        pe.wait_ge(sem("v"), pair + 1)
                    elif pair == 0:
                        pe.wait_ge(sem("v"), 3)
                    else:
                        pe.wait_ge(sem("v_last"), 1)
                    for s in range(NS):
                        lag = PH * PA * s
                        mm = pe.matmul(acc[:, :, lag:T], g[:, PA * s:PA * s + PA, :].rearrange("p a e -> p (a e)"),
                                       v2[:, part, 2 * pair:2 * pair + 2, 0:T - lag],
                                       start=(g is gl and s == 0), stop=(part == 1 and s == NS - 1),
                                       skip_group_check=True)
                mm.then_inc(sem("stu_psum"), 1)
            for a in range(PA):
                for b in range(B):
                    if a == 0 and b % 2 == 0:
                        pe.wait_ge(sem("stu"), b // 2 + 1)
                    mm = pe.matmul(chainB[32 * b:32 * b + 32, PH * a:T], ident[:, 32 * a:32 * a + 32],
                                   yb[:, b, 0:T - PH * a], start=False, stop=(a == PA - 1), skip_group_check=True)
            mm.then_inc(sem("back"), 1)

        @block.vector
        def _(dve):
            step = [0]

            def link(ins):
                step[0] += 1
                ins.then_inc(sem("dve_step"), 1)
                dve.wait_ge(sem("dve_step"), step[0])

            def mark(ins):
                step[0] += 1
                ins.then_inc(sem("dve_step"), 1)

            def settle():
                dve.wait_ge(sem("dve_step"), step[0])

            def g_low(name):
                for q in spots(name):
                    dve.wait_ge(sem("g_high"), q + 1)
                    dve.tensor_tensor(gl[:, :, EG * q:EG * q + EG].rearrange("p m e -> p e m"),
                                      gbank[q % 2][:, :].rearrange("p (e m) -> p e m", e=EG),
                                      gh[:, :, EG * q:EG * q + EG].rearrange("p m e -> p e m"),
                                      ALU.subtract).then_inc(sem("g_low"), 1)

            def block_of(b, src):
                r = slice(32 * b, 32 * b + 32)
                dve.tensor_copy(blk[r, b, :], src[r, :]).then_inc(sem("blk_v"), 1)

            for n, v in enumerate((GN_EPS, BN_EPS, LN_EPS, LN_EPS * USCALE ** -2)):
                ins = dve.memset(eps[:, n:n + 1], v)
            ins.then_inc(sem("eps"), 1)
            dve.memset(busy[:, :], 1.0).then_inc(sem("busy"), 1)
            dve.wait_ge(sem("x_in"), 16)
            link(dve.bn_stats(rs6[:, :], x_sb[:, :]))
            dve.bn_aggr(st[:, 0:2], rs6[:, :]).then_inc(sem("gn_mv"), 1)
            dve.wait_ge(sem("gn_std"), 1)
            link(dve.reciprocal(grstd, gstd))
            dve.tensor_scalar(h[:, :], x_sb[:, :], mean, grstd, ALU.subtract, ALU.mult).then_inc(sem("h"), 1)
            dve.wait_ge(sem("h"), 1)
            dve.wait_ge(sem("zero"), 1)
            block_of(0, h)
            dve.tensor_tensor(hsq[:, :], h[:, :], h[:, :], ALU.mult).then_inc(sem("hsq"), 1)
            dve.wait_ge(sem("small_in"), 16)
            mark(dve.tensor_tensor(logits, sml[:, P_LOGW:P_LOGW + NX], sml[:, P_GUMBEL:P_GUMBEL + NX], ALU.add))
            dve.wait_ge(sem("hsq"), 1)
            dve.wait_ge(sem("hsq_high"), 1)
            dve.tensor_tensor(hq[:, 1, :], hsq[:, :], hq[:, 0, :], ALU.subtract).then_inc(sem("hsq_low"), 1)
            settle()
            mark(dve.reduce_max(lmax, logits, AX_X))
            block_of(1, h)
            settle()
            dve.tensor_scalar(ranked, logits, lmax, None, ALU.subtract).then_inc(sem("logits"), 1)
            dve.wait_ge(sem("phi_in"), 16)
            dve.tensor_reduce(amax[:, 0:1], phi_sb[:, :], AX_X, ALU.max, apply_absolute_value=True)\
               .then_inc(sem("amax"), 1)
            dve.wait_ge(sem("sqi_psum"), 1)
            dve.tensor_scalar(thr[:, :, :].rearrange("p h b -> p (h b)"), gbank[0][:, 0:2 * B], -1.0, RADIUS2 / 2,
                              ALU.mult, ALU.add).then_inc(sem("thr"), 1)

            def compare(b, n):
                dve.wait_ge(sem("sqj"), b // 2 + 1)
                dve.wait_ge(sem("gram"), b + 1)
                dve.scalar_tensor_tensor(out=hgraph[:, b, n, :], in0=quad[:, b, n * T:(n + 1) * T],
                                         scalar=thr[:, n, b:b + 1], in1=sqj[:, b, :],
                                         op0=ALU.add, op1=ALU.is_gt, accum_out=deg[:, n, b:b + 1])\
                   .then_inc(sem("compare"), 1)

            dve.wait_ge(sem("thr"), 1)
            compare(0, 0)
            compare(0, 1)
            dve.wait_ge(sem("xe_psum"), 1)
            dve.tensor_tensor(xe[:, :, :], gbank[1][:, 0:2 * P].rearrange("p (h f) -> p h f", h=2),
                              sml[:, P_BIAS:P_BIAS + P].unsqueeze(1).broadcast_to([P, 2, P]), ALU.add)\
               .then_inc(sem("xe"), 1)
            compare(1, 0)
            dve.wait_ge(sem("expl"), 1)
            mark(dve.reciprocal(lrec, lsum))
            compare(1, 1)
            settle()
            mark(dve.tensor_scalar(soft, expl, lrec, None, ALU.mult))
            compare(2, 0)
            settle()
            mark(dve.reduce_max(smax, soft, AX_X))
            compare(2, 1)
            settle()
            mark(dve.scalar_tensor_tensor(out=ranked, in0=soft, scalar=smax, in1=sml[:, P_RANK:P_RANK + NX],
                                          op0=ALU.is_equal, op1=ALU.mult))
            compare(3, 0)
            settle()
            mark(dve.reduce_max(fmax, ranked, AX_X))
            compare(3, 1)
            dve.wait_ge(sem("compare"), 2 * B)
            mark(dve.tensor_scalar(deg[:, :, :], deg[:, :, :], 1.0, None, ALU.max))
            settle()
            dve.tensor_scalar(onehot, ranked, fmax, None, ALU.is_equal).then_inc(sem("onehot"), 1)
            dve.reciprocal(rdeg[:, :, :], deg[:, :, :]).then_inc(sem("rdeg"), 1)
            link(dve.scalar_tensor_tensor(out=wts, in0=ranked, scalar=fmax, in1=soft,
                                          op0=ALU.is_equal, op1=ALU.subtract))
            dve.tensor_tensor(wts, wts, soft, ALU.add).then_inc(sem("wts"), 1)
            dve.wait_ge(sem("gmaxp"), 1)
            link(dve.tensor_scalar(bnd, gmaxp[:, :], TINY, None, ALU.max))
            link(dve.tensor_scalar(p2_phi.bitcast(I32), bnd.bitcast(I32), 0x7F800000, None, ALU.bitwise_and))
            link(dve.reciprocal(sc_phi, p2_phi))
            dve.tensor_scalar(sc_phi, sc_phi, PTOP / 2, None, ALU.mult).then_inc(sem("scale_phi"), 1)
            dve.wait_ge(sem("wts"), 1)
            dve.wait_ge(sem("sig"), 2)
            mark(dve.scalar_tensor_tensor(out=wsum[:, :], in0=wts, scalar=sig, in1=sml[:, P_EXPERT:P_EXPERT + NX],
                                          op0=ALU.mult, op1=ALU.mult, accum_out=ws))
            dve.wait_ge(sem("rdeg"), 1)
            dve.wait_ge(sem("edget_psum"), 1)
            dve.tensor_tensor(edget[:, :, :, :], chainB[:, 0:T].rearrange("p (h b c) -> p h b c", h=2, b=B),
                              rdeg[:, :, :].unsqueeze(3).broadcast_to([P, 2, B, C]), ALU.mult)\
               .then_inc(sem("edget"), 1)
            dve.wait_ge(sem("m_in"), 16)
            mark(dve.tensor_reduce(amax[:, 3:4], m_sb[:, :], AX_X, ALU.max, apply_absolute_value=True))
            settle()
            dve.tensor_tensor(amax[:, 1:2], amax[:, 3:4], ws, ALU.mult).then_inc(sem("amax"), 1)
            dve.wait_ge(sem("mumix"), 1)
            dve.tensor_reduce(amax[:, 2:3], mumix[:, :], AX_X, ALU.max, apply_absolute_value=True)\
               .then_inc(sem("amax"), 1)
            dve.wait_ge(sem("vert_psum"), 1)
            dve.wait_ge(sem("rdegc"), 1)
            link(dve.tensor_tensor(conv[:, :], quad[:, 0, 0:T], rdegc[:, :], ALU.mult))
            link(dve.tensor_tensor(conv[:, :], conv[:, :], h[:, :], ALU.add))
            link(dve.bn_stats(cs6[:, :], conv[:, :]))
            dve.tensor_tensor(bnst[:, :, :], cst[:, BMASK:BMASK + B * 6].rearrange("p (b s) -> p b s", b=B),
                              cs6[:, :].unsqueeze(1).broadcast_to([P, B, 6]), ALU.mult).then_inc(sem("bnst"), 1)
            dve.wait_ge(sem("gmaxm"), 1)
            link(dve.tensor_tensor(bnd, gmaxm[:, 1:2], sc_phi, ALU.mult))
            link(dve.scalar_tensor_tensor(out=bnd, in0=bnd, scalar=1.0 / PTOP ** 2, in1=gmaxm[:, 0:1],
                                          op0=ALU.mult, op1=ALU.max))
            mark(dve.tensor_scalar(bnd, bnd, TINY, None, ALU.max))
            dve.wait_ge(sem("bn_psum"), 1)
            dve.bn_aggr(bnaff[:, 0:2], chainB[:, 0:B * 6]).then_inc(sem("bn_mv"), 1)
            settle()
            link(dve.tensor_scalar(p2_m.bitcast(I32), bnd.bitcast(I32), 0x7F800000, None, ALU.bitwise_and))
            mark(dve.reciprocal(sc_m, p2_m))
            dve.wait_ge(sem("bn_std"), 1)
            mark(dve.reciprocal(brstd, bstd))
            settle()
            dve.tensor_scalar(sc_m, sc_m, PTOP / 2, None, ALU.mult).then_inc(sem("scale"), 1)
            link(dve.tensor_tensor(ba, brstd, sml[:, P_GAMMA:P_GAMMA + 1], ALU.mult))
            link(dve.scalar_tensor_tensor(out=bb, in0=ba, scalar=bnaff[:, 0:1], in1=sml[:, P_BETA:P_BETA + 1],
                                          op0=ALU.mult, op1=ALU.subtract))
            dve.tensor_scalar(ba2, ba, 0.5, None, ALU.mult)
            dve.tensor_scalar(bb2, bb, -0.5, None, ALU.mult).then_inc(sem("halves"), 1)
            dve.tensor_scalar(y[:, :], conv[:, :], ba, bb, ALU.mult, ALU.subtract).then_inc(sem("y"), 1)
            dve.wait_ge(sem("scale"), 1)
            mark(dve.tensor_tensor(isc, p2_m, p2_phi, ALU.mult))
            mark(dve.tensor_tensor(ws, ws, sc_m, ALU.mult))
            settle()
            dve.tensor_scalar(isc, isc, 4.0 / PTOP ** 2 / USCALE, None, ALU.mult).then_inc(sem("scale_m"), 1)
            dve.tensor_scalar(rw[:, :], cst[:, REP_K:REP_K + P], ws, None, ALU.mult).then_inc(sem("rw"), 1)
            dve.wait_ge(sem("y"), 1)
            dve.wait_ge(sem("th"), 1)
            link(dve.scalar_tensor_tensor(out=th[:, :], in0=th[:, :], scalar=1.0, in1=y[:, :],
                                          op0=ALU.add, op1=ALU.mult))
            dve.scalar_tensor_tensor(out=x1[:, :], in0=th[:, :], scalar=0.5, in1=x_sb[:, :],
                                     op0=ALU.mult, op1=ALU.add).then_inc(sem("x1"), 1)
            for n in range(2):
                dve.wait_ge(sem("mst_high"), n + 1)
                lower = mst[P // 2:P, 16 * n:16 * n + 16, :].rearrange("p e d -> p (e d)")
                dve.tensor_tensor(lower, gbank[n][P // 2:P, :], lower, ALU.subtract).then_inc(sem("mst_low"), 1)

            def spread(src):
                link(dve.reciprocal(rstd[:, :], src))
                dve.tensor_copy(rstdb[:, :, :, :],
                                rstd[:, :].rearrange("p (h b) -> p h b", h=2).unsqueeze(3).broadcast_to([P, 2, B, C]))\
                   .then_inc(sem("rstdb"), 1)

            dve.wait_ge(sem("sq"), 1)
            dve.tensor_copy(xm[:, :], quad[:, 3, 0:T]).then_inc(sem("xm"), 1)
            g_low("silu")
            dve.wait_ge(sem("std"), 1)
            spread(std[:, :])
            g_low("ln1")
            dve.wait_ge(sem("xm"), 1)
            dve.wait_ge(sem("rstdc_psum"), 1)
            dve.tensor_tensor(z[:, :], xm[:, :], chainA[:, 0:T], ALU.mult).then_inc(sem("z"), 1)
            dve.wait_ge(sem("z"), 1)
            block_of(0, z)
            block_of(1, z)
            g_low("z")
            dve.wait_ge(sem("exp"), 2 * B)
            spread(den[:, :, :].rearrange("p h b -> p (h b)"))
            dve.wait_ge(sem("o"), 1)
            dve.wait_ge(sem("rden_psum"), 1)
            link(dve.tensor_tensor(t2[:, :], chainB[:, 0:T], o_sb[:, :], ALU.mult))
            dve.tensor_tensor(t2[:, :], t2[:, :], x1[:, :], ALU.add).then_inc(sem("t2"), 1)
            g_low("scores")
            dve.wait_ge(sem("sq"), 2)
            dve.tensor_copy(xm[:, :], quad[:, 3, 0:T]).then_inc(sem("xm"), 1)
            dve.wait_ge(sem("std"), 2)
            spread(std[:, :])
            dve.wait_ge(sem("xm"), 2)
            dve.wait_ge(sem("rstdc_psum"), 2)
            uh, ul = (u2[:, n, PAD:PAD + T] for n in range(2))
            dve.tensor_tensor(uh, xm[:, :], chainA[:, 0:T], ALU.mult).then_inc(sem("u_high"), 1)
            link(dve.tensor_tensor(u32[:, :], xm[:, :], chainA[:, 0:T], ALU.mult))
            dve.tensor_tensor(ul, u32[:, :], uh, ALU.subtract).then_inc(sem("u_low"), 1)
            dve.wait_ge(sem("v_psum"), 4)
            dve.tensor_copy(v2[:, 1, 2:4, :], quad[:, 3, :].rearrange("p (b t) -> p b t", b=2))\
               .then_inc(sem("v_last"), 1)
            dve.wait_ge(sem("mask"), NX + PA)
            for pair in range(2):
                dve.wait_ge(sem("stu_psum"), pair + 1)
                dve.tensor_tensor(yb[:, 2 * pair:2 * pair + 2, :], gbank[pair][:, :].rearrange("p (b t) -> p b t", b=2),
                                  maskp[:, :].unsqueeze(1).broadcast_to([P, 2, T]), ALU.mult).then_inc(sem("stu"), 1)
            dve.wait_ge(sem("back"), 1)
            dve.tensor_copy(res[:, :], chainB[:, 0:T]).then_inc(sem("res"), 1)


def constants():
    p = np.arange(P)
    group, chan = p // C, p % C
    same_group = group[:, None] == group[None, :]
    same_chan = chan[:, None] == chan[None, :]
    k = p % K
    minus = (p // K) % 2
    c = np.zeros((P, NCONST))
    c[:, IDENT:IDENT + P] = np.eye(P)
    c[:, CENTER:CENTER + P] = (same_chan - 1.0 / C) * same_group
    c[:, SAME_C:SAME_C + P] = same_chan
    c[:, REP_K:REP_K + P] = (k[:, None] == k[None, :]) & (minus[:, None] == minus[None, :])
    c[:, SIGN] = 1.0
    c[:, SIGN + 1] = 1.0 - 2.0 * minus
    c[:, COL32:COL32 + B] = (group[:, None] == np.arange(B)) / C
    c[:, BMASK:BMASK + B * 6] = np.repeat(group[:, None] == np.arange(B), 6, axis=1)
    return c.astype(np.float32)


def kernel(x, L0_conv_W_fc, L0_conv_b_fc, L0_conv_gamma, L0_conv_beta, L1_ffn_sigma, L1_ffn_phi, L1_ffn_M_u,
           L1_ffn_M_phi_plus, L1_ffn_M_phi_minus, L1_ffn_log_weights, L1_ffn_gumbel):
    import concourse.bacc as bacc
    from concourse.bass_utils import run_bass_kernel_spmd

    as_np = np.asarray
    small = np.zeros((P, NSMALL), np.float32)
    for b in range(B):
        small[32 * b:32 * b + 32, P_WT + 32 * b:P_WT + 32 * b + 32] = as_np(L0_conv_W_fc).T
    small[:, P_BIAS:P_BIAS + P] = np.tile(as_np(L0_conv_b_fc), B)
    small[:, P_GAMMA] = np.tile(as_np(L0_conv_gamma), B)
    small[:, P_BETA] = np.tile(as_np(L0_conv_beta), B)
    small[:, P_SIGMA] = np.tile(as_np(L1_ffn_sigma), P // K)
    small[:, P_LOGW:P_LOGW + NX] = as_np(L1_ffn_log_weights)
    small[:, P_GUMBEL:P_GUMBEL + NX] = as_np(L1_ffn_gumbel)
    small[:, P_EXPERT:P_EXPERT + NX] = np.repeat(np.eye(NX), P // NX, axis=0)
    small[:, P_RANK:P_RANK + NX] = np.arange(NX, 0, -1)
    mfilt = np.stack([as_np(L1_ffn_M_phi_plus), as_np(L1_ffn_M_phi_minus)], 1).transpose(0, 1, 2, 4, 3).reshape(P, C * C)
    phi4 = np.tile(as_np(L1_ffn_phi)[:T].T, (P // K, 1))
    mu = as_np(L1_ffn_M_u)
    mu4 = np.zeros((PH, C, NX, C), np.float32)
    mu4[:NTAU] = mu.transpose(1, 2, 0, 3)

    ins = {
        "in_x": np.ascontiguousarray(as_np(x)).reshape(P, T),
        "in_consts": constants(),
        "in_small": small,
        "in_mfilt": np.ascontiguousarray(mfilt),
        "in_phi": np.ascontiguousarray(phi4),
        "in_mu": mu4.reshape(P, NX * C),
    }
    nc = bacc.Bacc("TRN2", target_bir_lowering=False, num_devices=1)
    aps = [nc.dram_tensor(n, a.shape, mybir.dt.from_np(a.dtype), kind="ExternalInput").ap() for n, a in ins.items()]
    out = nc.dram_tensor("out", (P, T), F32, kind="ExternalOutput").ap()
    stu_hybrid_kernel(nc, *aps, out)
    r = run_bass_kernel_spmd(nc, [ins], core_ids=[0])
    return r.results[0]["out"].reshape(B, C, 16, 16)
```

```python
from contextlib import ExitStack

import numpy as np

import concourse.bass as bass
from concourse import mybir

ALU = mybir.AluOpType
ACT = mybir.ActivationFunctionType
F32 = mybir.dt.float32
F16 = mybir.dt.float16
I32 = mybir.dt.int32
AX_X = mybir.AxisListType.X
RMAX = bass.bass_isa.ReduceOp.max

B, C, T = 4, 32, 256
P = B * C
HT = T // 2
NX = 4
K = 16
NTAU = 3
PH = P // C
PA = P // C
NM = T // PH
NS = NM // PA
NG = 4
EG = C // NG
PAD = PH
BN_EPS = 1e-5
GN_EPS = 1e-5
LN_EPS = 1e-5
RADIUS2 = 16.0 ** 2
USCALE = 256.0
PTOP = 16.0
TINY = 1e-15

IDENT, CENTER, SAME_C, REP_K = (n * P for n in range(4))
SIGN = 4 * P
COL32 = SIGN + 2
BMASK = COL32 + B
NCONST = BMASK + B * 6
P_WT, P_BIAS, P_GAMMA, P_BETA, P_SIGMA, P_LOGW, P_GUMBEL = 0, P, P + 1, P + 2, P + 3, P + 4, P + 8
P_EXPERT = P_GUMBEL + NX
P_RANK = P_EXPERT + NX
NSMALL = P_RANK + NX

WARM_START, WARM_BN, WARM_Z, WARM_VAR = 7, 4, 4, 1


def stu_hybrid_kernel(nc, x, consts, small, mfilt, phi, mu, out):
    with ExitStack() as ctx:
        def sb(name, shape, dt=F32):
            return ctx.enter_context(nc.sbuf_tensor(name, shape, dt))

        sems = {}

        def sem(name):
            if name not in sems:
                sems[name] = ctx.enter_context(nc.semaphore("s_" + name))
            return sems[name]

        bank = [ctx.enter_context(nc.psum_tensor(f"bank{i}", [P, 512], F32)) for i in range(4)]
        quad = ctx.enter_context(nc.psum_tensor("quad", [P, 4, 512], F32))
        chainA, chainB, gbank = bank[0], bank[1], (bank[2][:, :], bank[3][:, :])

        x_sb = sb("x_sb", [P, T])
        cst = sb("cst", [P, NCONST])
        ident16 = sb("ident16", [P, P], F16)
        sml = sb("sml", [P, NSMALL])
        m_sb = sb("m_sb", [P, C * C])
        phi_sb = sb("phi_sb", [P, T])
        phis = sb("phis", [P, T])
        mu_sb = sb("mu_sb", [P, NX, C])
        mumix = sb("mumix", [P, NX, C])
        mtap = sb("mtap", [P, C])
        halfblk = sb("halfblk", [P, B, P], F16)
        hq = sb("hq", [P, 2, T], F16)
        busy = sb("busy", [P, 512], F16)
        spare = sb("spare", [P, 8])
        cover = sb("cover", [P, NX])
        mask0 = sb("mask0", [P, T + PH * PA])
        maskp = sb("maskp", [P, T])
        eps = sb("eps", [P, 4])
        lg = sb("lg", [P, 6 * NX])
        tiny = sb("tiny", [P, 32])
        wsum = sb("wsum", [P, 2, NX])
        rw = sb("rw", [P, P])
        amaxp = sb("amaxp", [P, 1])
        amaxm = sb("amaxm", [P, 2])
        rowmax = sb("rowmax", [P, 1])
        mumax = sb("mumax", [P, NX])
        gmaxp = sb("gmaxp", [P, 1])
        gmaxm = sb("gmaxm", [P, 2])
        mst = sb("mst", [P, C, C], F16)
        phst = sb("phst", [P, T], F16)
        gh = sb("gh", [P, NM, C], F16)
        gl = sb("gl", [P, NM, C], F16)
        g0 = sb("g0", [P, C])
        st = sb("st", [P, 8])
        h = sb("h", [P, T])
        blk = sb("blk", [P, B, T])
        hsq = sb("hsq", [P, T])
        thr = sb("thr", [P, 2, B])
        sqj = sb("sqj", [P, 2, T])
        hb = sb("hb", [P, T])
        hgraph = sb("hgraph", [P, B, 2, T])
        deg = sb("deg", [P, 2, B])
        rdeg = sb("rdeg", [P, 2, B])
        rdegc = sb("rdegc", [P, T])
        xe = sb("xe", [P, 2, P])
        edgec = sb("edgec", [P, T])
        edget = sb("edget", [P, 2, B, C])
        conv = sb("conv", [P, T])
        bnst = sb("bnst", [P, B, 6])
        y = sb("y", [P, T])
        th = sb("th", [P, T])
        silu = sb("silu", [P, T])
        x1 = sb("x1", [P, T])
        wo = sb("wo", [P, T])
        xm = sb("xm", [P, T])
        sq = sb("sq", [P, T])
        std = sb("std", [P, 8])
        rstd = sb("rstd", [P, 8])
        z = sb("z", [P, T])
        zt = sb("zt", [P, 2, B, C])
        e_sb = sb("e_sb", [P, B, 2, T])
        den = sb("den", [P, 2, B])
        o_sb = sb("o_sb", [P, T])
        t2 = sb("t2", [P, T])
        u32 = sb("u32", [P, T])
        u2 = sb("u2", [P, 2, PAD + T], F16)
        v2 = sb("v2", [P, 2, B, T], F16)
        yb = sb("yb", [P, B, T])
        res = sb("res", [P, T])

        ident = cst[:, IDENT:IDENT + P]
        logits, expl, soft, ranked, wts, onehot = (lg[:, n * NX:(n + 1) * NX] for n in range(6))
        lmax, lsum, smax, ws, sig, sc_m, isc, p2_m, sc_phi, p2_phi, lrec, bnd, fmax = \
            (tiny[:, n:n + 1] for n in range(13))
        mean, var, gstd, grstd = (st[:, n:n + 1] for n in range(4))
        bnaff = sb("bnaff", [P, 9])
        bstd, brstd, ba2, bb2, gamma2, beta2, nmean = (bnaff[:, n + 2:n + 3] for n in range(7))
        rs6 = sb("rs6", [P, 6])
        cs6 = sb("cs6", [P, 6])

        block = ctx.enter_context(nc.Block())

        mixbank = (gbank[0], quad[:, 1, :])
        gacc = (gbank[0], gbank[1], quad[:, 2, :], quad[:, 3, :])

        @block.sync
        def _(sp):
            sp.dma_start(x_sb[:, :], x).then_inc(sem("x_in"), 16)
            sp.dma_start(phi_sb[:, :], phi).then_inc(sem("phi_in"), 16)
            sp.dma_start(m_sb[:, :], mfilt).then_inc(sem("m_in"), 16)
            sp.dma_start(cst[:, :], consts).then_inc(sem("const_in"), 16)
            sp.dma_start(mu_sb[:, :, :], mu.rearrange("p (i f) -> p i f", i=NX)).then_inc(sem("mu_in"), 16)
            sp.wait_ge(sem("res"), 1)
            sp.dma_start(out, res[:, :]).then_inc(sem("out"), 16)
            sp.wait_ge(sem("out"), 16)

        @block.gpsimd
        def _(pool):
            step = [0]

            def link(ins):
                step[0] += 1
                ins.then_inc(sem("pool_step"), 1)
                pool.wait_ge(sem("pool_step"), step[0])

            link(pool.memset(halfblk[:, :, :], 0.0))
            for b in range(B):
                pool.memset(halfblk[32 * b:32 * b + 32, b, :], -0.5).then_inc(sem("halfblk"), 1)
            pool.wait_ge(sem("halfblk"), B)
            pool.memset(blk[:, :, :], 0.0).then_inc(sem("zero"), 1)
            pool.memset(u2[:, :, 0:PAD], 0.0).then_inc(sem("zero"), 1)
            pool.wait_ge(sem("amaxp"), 1)
            pool.wait_ge(sem("zero"), 2)
            pool.partition_all_reduce(gmaxp[:, :], amaxp[:, :], P, RMAX).then_inc(sem("gmaxp"), 1)
            pool.wait_ge(sem("small_in"), 16)
            pool.wait_ge(sem("h"), 1)
            pool.wait_ge(sem("gmaxp"), 1)
            pool.tensor_scalar(hb[:, :], h[:, :], sml[:, P_BIAS:P_BIAS + 1], 0.0, ALU.add, ALU.add)\
                .then_inc(sem("hb"), 1)
            pool.wait_ge(sem("const_in"), 16)
            pool.wait_ge(sem("scale_phi"), 1)
            pool.wait_ge(sem("hb"), 1)
            link(pool.tensor_scalar(phis[:, :], phi_sb[:, :], sc_phi, 0.0, ALU.mult, ALU.add))
            link(pool.tensor_tensor(phis[:, :].rearrange("p (m s) -> p m s", s=2),
                                    phis[:, :].rearrange("p (m s) -> p m s", s=2),
                                    cst[:, SIGN:SIGN + 2].unsqueeze(1).broadcast_to([P, HT, 2]), ALU.mult))
            link(pool.tensor_scalar(phst[:, :], phis[:, :], 1.0, 0.0, ALU.mult, ALU.add))
            for g in (1, 3):
                r = slice(32 * g, 32 * g + 32)
                pool.tensor_tensor(phst[r, :], phis[r, :], phst[r, :], ALU.subtract).then_inc(sem("phst"), 1)
            pool.wait_ge(sem("amaxm"), 2)
            pool.wait_ge(sem("phst"), 2)
            pool.partition_all_reduce(gmaxm[:, :], amaxm[:, :], P, RMAX).then_inc(sem("gmaxm"), 1)
            pool.wait_ge(sem("mu_in"), 16)
            pool.wait_ge(sem("wts"), 1)
            pool.wait_ge(sem("gmaxm"), 1)
            link(pool.tensor_tensor(mumix[:, :, :], mu_sb[:, :, :], wts.unsqueeze(2).broadcast_to([P, NX, C]),
                                    ALU.mult))
            link(pool.tensor_tensor(mumix[:, 0:2, :], mumix[:, 0:2, :], mumix[:, 2:4, :], ALU.add))
            link(pool.tensor_tensor(mtap[:, :], mumix[:, 0, :], mumix[:, 1, :], ALU.add))
            pool.wait_ge(sem("scale_m"), 2)
            link(pool.tensor_scalar(mtap[:, :], mtap[:, :], sc_m, 0.0, ALU.mult, ALU.add))
            link(pool.tensor_scalar(mtap[:, :], mtap[:, :], sc_phi, 0.0, ALU.mult, ALU.add))
            pool.wait_ge(sem("onehot"), 1)
            link(pool.tensor_scalar(cover[:, :], onehot, isc, 0.0, ALU.mult, ALU.add))
            for i in range(1, NX):
                link(pool.tensor_tensor(cover[:, i:i + 1], cover[:, i:i + 1], cover[:, i - 1:i], ALU.add))
            link(pool.memset(mask0[:, :], 0.0))
            for i in range(NX):
                lo = 0 if i == NX - 1 else T >> (i + 1)
                seg = mask0[:, lo:T >> i]
                pool.tensor_scalar(seg, seg, cover[:, i:i + 1], 0.0, ALU.add, ALU.add).then_inc(sem("mask"), 1)
            pool.wait_ge(sem("mask"), NX)
            for a in range(PA):
                r = slice(32 * a, 32 * a + 32)
                pool.tensor_scalar(maskp[r, :], mask0[r, PH * a:PH * a + T], 1.0, 0.0, ALU.mult, ALU.add)\
                    .then_inc(sem("mask"), 1)
            for q in range(NG):
                pool.wait_ge(sem(f"g_low{q}"), 1)
            pool.wait_ge(sem("mask"), NX + PA)
            link(pool.tensor_tensor(g0[:, :], gh[:, 0, :], gl[:, 0, :], ALU.add))
            link(pool.tensor_tensor(g0[:, :], g0[:, :], mtap[:, :], ALU.add))
            link(pool.tensor_scalar(gh[:, 0, :], g0[:, :], 1.0, 0.0, ALU.mult, ALU.add))
            pool.tensor_tensor(gl[:, 0, :], g0[:, :], gh[:, 0, :], ALU.subtract).then_inc(sem("g_ready"), 1)

        @block.scalar
        def _(act):
            act.dma_start(sml[:, :], small).then_inc(sem("small_in"), 16)

            loads = []

            def tables(func):
                loads.append(func)
                act.activation(spare[:, len(loads) - 1:len(loads)], eps[:, 0:1], func)

            def g_high(q):
                act.wait_ge(sem("g_psum"), q + 1)
                act.activation(gh[:, :, EG * q:EG * q + EG].rearrange("p m e -> p e m"),
                               gacc[q].rearrange("p (e m) -> p e m", e=EG), ACT.Copy)\
                   .then_inc(sem(f"g_high{q}"), 1)

            act.wait_ge(sem("eps"), 1)
            tables(ACT.Sqrt)
            act.wait_ge(sem("gn_mv"), 1)
            act.activation(gstd, var, ACT.Sqrt, bias=eps[:, 0:1]).then_inc(sem("gn_std"), 1)
            act.wait_ge(sem("small_in"), 16)
            act.activation(sig, sml[:, P_SIGMA:P_SIGMA + 1], ACT.Sqrt).then_inc(sem("sig"), 1)
            act.wait_ge(sem("sig"), 1)
            act.activation(sig, sig, ACT.Sqrt).then_inc(sem("sig"), 1)
            act.wait_ge(sem("h"), 1)
            act.activation(hq[:, 0, :], h[:, :], ACT.Square).then_inc(sem("hsq_high"), 1)
            act.activation(hsq[:, :], h[:, :], ACT.Square).then_inc(sem("hsq"), 1)
            act.wait_ge(sem("zero"), 1)
            for b in (2, 3):
                r = slice(32 * b, 32 * b + 32)
                act.activation(blk[r, b, :], h[r, :], ACT.Copy).then_inc(sem("blk_a"), 1)
            act.wait_ge(sem("logits"), 1)
            act.activation(expl, ranked, ACT.Exp, accum_out=lsum).then_inc(sem("expl"), 1)
            tables(ACT.Sqrt)
            act.wait_ge(sem("sqj_psum"), 1)
            act.activation(sqj[:, :, :], chainB[:, :].rearrange("p (b t) -> p b t", b=2), ACT.Copy, scale=-1.0)\
               .then_inc(sem("sqj"), 1)
            act.wait_ge(sem("xe_psum"), 1)
            act.activation(xe[:, :, :], gbank[1][:, 0:2 * P].rearrange("p (h f) -> p h f", h=2), ACT.Copy)\
               .then_inc(sem("xe"), 1)
            act.wait_ge(sem("const_in"), 16)
            act.activation(ident16[:, :], ident, ACT.Copy).then_inc(sem("ident16"), 1)
            act.wait_ge(sem("edge_psum"), 1)
            act.activation(edgec[:, :], chainA[:, 0:T], ACT.Copy).then_inc(sem("edgec"), 1)
            act.wait_ge(sem("rdegc_psum"), 1)
            act.activation(rdegc[:, :], chainA[:, 0:T], ACT.Copy).then_inc(sem("rdegc"), 1)
            for n in range(2):
                act.wait_ge(sem("mix_psum"), n + 1)
                act.activation(mst[:, 16 * n:16 * n + 16, :], mixbank[n].rearrange("p (e d) -> p e d", d=C),
                               ACT.Copy).then_inc(sem("mst_high"), 1)
            act.wait_ge(sem("bn_mv"), 1)
            act.activation(bstd, bnaff[:, 1:2], ACT.Sqrt, bias=eps[:, 1:2]).then_inc(sem("bn_std"), 1)
            tables(ACT.Exp)
            act.wait_ge(sem("halves"), 1)
            act.activation(th[:, :], conv[:, :], ACT.Tanh, scale=ba2, bias=bb2).then_inc(sem("th"), 1)
            tables(ACT.Sqrt)
            act.wait_ge(sem("xm_psum"), 1)
            act.activation(sq[:, :], quad[:, 0, 0:T], ACT.Square).then_inc(sem("sq"), 1)
            g_high(0)
            act.wait_ge(sem("var_psum"), 1)
            act.activation(std[:, :], chainA[:, T:T + 2 * B], ACT.Sqrt, bias=eps[:, 2:3]).then_inc(sem("std"), 1)
            tables(ACT.Exp)
            g_high(2)
            g_high(3)
            act.wait_ge(sem("zt_psum"), 1)
            act.activation(zt[:, :, :, :].rearrange("p h b c -> p (h b c)"), chainB[:, 0:T], ACT.Copy)\
               .then_inc(sem("zt"), 1)
            for b in range(B):
                act.wait_ge(sem("scores"), b + 1)
                for n in range(2):
                    act.activation(e_sb[:, b, n, :], quad[:, b, n * T:(n + 1) * T], ACT.Exp,
                                   accum_out=den[:, n, b:b + 1]).then_inc(sem("exp"), 1)
            act.wait_ge(sem("av"), 1)
            act.activation(o_sb[:, :], chainA[:, 0:T], ACT.Copy).then_inc(sem("o"), 1)
            tables(ACT.Sqrt)
            act.wait_ge(sem("xm_psum"), 2)
            act.activation(sq[:, :], quad[:, 0, 0:T], ACT.Square).then_inc(sem("sq"), 1)
            act.wait_ge(sem("var_psum"), 2)
            act.activation(std[:, :], chainA[:, T:T + 2 * B], ACT.Sqrt, bias=eps[:, 3:4], scale=USCALE ** -2)\
               .then_inc(sem("std"), 1)
            for b in (0, 2, 3):
                act.wait_ge(sem("v_psum"), b + 1)
                act.activation(v2[:, 0, b, :], quad[:, b, 0:T], ACT.Copy).then_inc(sem("v_act"), 1)
            act.wait_ge(sem("v_psum"), 6)
            act.activation(v2[:, 1, 0:2, :], quad[:, 0, :].rearrange("p (b t) -> p b t", b=2), ACT.Copy)\
               .then_inc(sem("v_act"), 1)

        @block.tensor
        def _(pe):
            def g_psum(n):
                pe.wait_ge(sem("phst"), 2)
                pe.wait_ge(sem("mst_low"), n // 2 + 1)
                for e in range(EG):
                    for q in range(PH):
                        mm = pe.matmul(gacc[n][32 * q:32 * q + 32, NM * e:NM * e + NM],
                                       mst[:, EG * n + e, :], phst[:, q:T:PH], start=True, stop=True)
                mm.then_inc(sem("g_psum"), 1)

            def keep_busy(dst, count):
                for _ in range(count):
                    pe.matmul(dst, busy[:, 0:P], busy[:, :], start=True, stop=True)

            def turn(dst, src, signal):
                for n in range(2):
                    mm = pe.transpose(dst[:, n * P:(n + 1) * P], src[:, n * P:(n + 1) * P], ident)
                mm.then_inc(sem(signal), 1)

            def turn_rows(dst, rows, signal):
                for n in range(2):
                    for b in range(B):
                        mm = pe.matmul(dst[32 * b:32 * b + 32, n * P:(n + 1) * P],
                                       rows[:, n * B + b:n * B + b + 1].broadcast_to([P, C]), ident,
                                       start=True, stop=True)
                mm.then_inc(sem(signal), 1)

            def gram(b):
                pe.wait_ge(sem("blk_v" if b < 2 else "blk_a"), b % 2 + 1)
                for n in range(2):
                    mm = pe.matmul(quad[:, b, n * T:(n + 1) * T], blk[:, b, n * HT:(n + 1) * HT], h[:, :],
                                   start=True, stop=(b >= 2))
                    if b < 2:
                        if b == 0 and n == 0:
                            pe.wait_ge(sem("hsq_high"), 1)
                            pe.wait_ge(sem("hsq_low"), 1)
                            pe.wait_ge(sem("halfblk"), B)
                        for part in range(2):
                            mm = pe.matmul(quad[:, b, n * T:(n + 1) * T], halfblk[:, b, :], hq[:, part, :],
                                           start=False, stop=(part == 1))
                mm.then_inc(sem("gram"), 1)

            def mix(n):
                pe.matmul(mixbank[n], rw[:, :], m_sb[:, 512 * n:512 * n + 512], start=True, stop=True)\
                  .then_inc(sem("mix_psum"), 1)

            def edge_sums(b):
                pe.wait_ge(sem("compare"), 2 * b + 2)
                for n in range(2):
                    mm = pe.matmul(chainA[32 * b:32 * b + 32, 0:T], xe[:, n, 32 * b:32 * b + 32], hgraph[:, b, n, :],
                                   start=(n == 0), stop=(n == 1))
                return mm

            pe.wait_ge(sem("busy"), 1)
            keep_busy(gbank[1], WARM_START)
            pe.wait_ge(sem("h"), 1)
            gram(0)
            for n in range(2):
                for part in range(2):
                    mm = pe.matmul(gbank[0][:, n * B:(n + 1) * B], hq[:, part, n * HT:(n + 1) * HT],
                                   halfblk[:, :, 0], start=(part == 0), stop=(part == 1))
            mm.then_inc(sem("sqi_psum"), 1)
            gram(1)
            for b in (2, 3):
                for part in range(2):
                    mm = pe.matmul(chainB[:, (b - 2) * T:(b - 1) * T], halfblk[:, b, :], hq[:, part, :],
                                   start=(part == 0), stop=(part == 1))
            mm.then_inc(sem("sqj_psum"), 1)
            gram(2)
            pe.wait_ge(sem("small_in"), 16)
            for n in range(2):
                mm = pe.matmul(gbank[1][:, n * P:(n + 1) * P], h[:, n * HT:(n + 1) * HT], sml[:, P_WT:P_WT + P],
                               start=True, stop=True)
            mm.then_inc(sem("xe_psum"), 1)
            gram(3)
            pe.wait_ge(sem("xe"), 1)
            for b in range(B):
                mm = edge_sums(b)
            mm.then_inc(sem("edge_psum"), 1)
            pe.wait_ge(sem("const_in"), 16)
            pe.wait_ge(sem("edgec"), 1)
            turn(chainB, edgec, "edget_psum")
            pe.wait_ge(sem("rdeg"), 1)
            turn_rows(chainA, rdeg[:, :, :].rearrange("p h b -> p (h b)"), "rdegc_psum")
            pe.wait_ge(sem("edget"), 1)
            for n in range(2):
                for b in range(B):
                    mm = pe.matmul(quad[32 * b:32 * b + 32, 0, 0:T], edget[:, n, b, :], hgraph[:, b, n, :],
                                   start=(n == 0), stop=(n == 1))
            mm.then_inc(sem("vert_psum"), 1)
            pe.wait_ge(sem("m_in"), 16)
            pe.wait_ge(sem("rw"), 1)
            pe.wait_ge(sem("thr"), 1)
            mix(0)
            mix(1)
            pe.wait_ge(sem("bnst"), 1)
            pe.matmul(chainB[:, 0:B * 6], cst[:, SAME_C:SAME_C + P], bnst[:, :, :].rearrange("p b s -> p (b s)"),
                      start=True, stop=True).then_inc(sem("bn_psum"), 1)
            g_psum(0)
            g_psum(1)
            pe.wait_ge(sem("vert"), 1)
            pe.matmul(quad[:, 0, 0:T], cst[:, CENTER:CENTER + P], x_sb[:, :], start=True, stop=False)
            pe.wait_ge(sem("bn_mv"), 1)
            keep_busy(chainB[:, :], WARM_BN)
            pe.wait_ge(sem("silu"), 1)
            pe.matmul(quad[:, 0, 0:T], cst[:, CENTER:CENTER + P], silu[:, :], start=False, stop=True)\
              .then_inc(sem("xm_psum"), 1)
            g_psum(2)

            def variance(n_th):
                pe.wait_ge(sem("sq"), n_th)
                for n in range(2):
                    mm = pe.matmul(chainA[:, T + n * B:T + (n + 1) * B], sq[:, n * P:(n + 1) * P],
                                   cst[:, COL32:COL32 + B], start=True, stop=True)
                mm.then_inc(sem("var_psum"), 1)

            variance(1)
            g_psum(3)
            pe.wait_ge(sem("rstd"), 1)
            turn_rows(chainA, rstd, "rstdc_psum")
            keep_busy(chainB[:, :], WARM_Z)
            pe.wait_ge(sem("z"), 1)
            for b in range(B):
                if b == 1:
                    turn(chainB, z, "zt_psum")
                if b >= 2:
                    pe.wait_ge(sem(f"g_low{b}"), 1)
                r = slice(32 * b, 32 * b + 32)
                for n in range(2):
                    mm = pe.matmul(quad[:, b, n * T:(n + 1) * T], z[r, n * HT:(n + 1) * HT], z[r, :],
                                   start=True, stop=True)
                mm.then_inc(sem("scores"), 1)
            pe.wait_ge(sem("zt"), 1)
            for b in range(B):
                pe.wait_ge(sem("exp"), 2 * b + 2)
                for n in range(2):
                    mm = pe.matmul(chainA[32 * b:32 * b + 32, 0:T], zt[:, n, b, :], e_sb[:, b, n, :],
                                   start=(n == 0), stop=(n == 1))
            mm.then_inc(sem("av"), 1)
            pe.wait_ge(sem("rstd"), 2)
            turn_rows(chainB, rstd, "rden_psum")
            pe.wait_ge(sem("x1"), 1)
            pe.matmul(quad[:, 0, 0:T], cst[:, CENTER:CENTER + P], x1[:, :], start=True, stop=False)
            pe.wait_ge(sem("wo"), 1)
            pe.matmul(quad[:, 0, 0:T], cst[:, CENTER:CENTER + P], wo[:, :], start=False, stop=True)\
              .then_inc(sem("xm_psum"), 1)
            variance(2)
            pe.wait_ge(sem("t2"), 1)
            pe.matmul(chainB[:, 0:T], ident, t2[:, :], start=True, stop=False, skip_group_check=True)
            pe.wait_ge(sem("g_low1"), 1)
            keep_busy(gbank[1], WARM_VAR)
            pe.wait_ge(sem("rstd"), 3)
            turn_rows(chainA, rstd, "rstdc_psum")
            pe.wait_ge(sem("ident16"), 1)
            pe.wait_ge(sem("zero"), 2)
            pe.wait_ge(sem("xm"), 2)

            def to_phases(part, b, dst):
                for q in range(PH):
                    mm = pe.matmul(dst[32 * q:32 * q + 32, :], ident16[:, 32 * b:32 * b + 32],
                                   u2[:, part, PAD - q:PAD - q + T], start=True, stop=True)
                mm.then_inc(sem("v_psum"), 1)

            def convolve(half, g, part, batches=range(B), first=False, last=False):
                acc = gbank[half].rearrange("p (b t) -> p b t", b=B)
                bs = slice(batches[0], batches[-1] + 1)
                steps = NS // 2 * (half + 1)
                for s in range(steps):
                    begin = HT * half - PH * PA * s
                    lag = max(0, -begin)
                    mm = pe.matmul(acc[:, bs, lag:HT], g[:, PA * s:PA * s + PA, :].rearrange("p a e -> p (a e)"),
                                   v2[:, part, bs, begin + lag:begin + HT],
                                   start=(first and s == 0), stop=(last and s == steps - 1), skip_group_check=True)
                if last:
                    mm.then_inc(sem("stu_psum"), 1)

            pe.wait_ge(sem("u_high"), 1)
            for b in range(B):
                to_phases(0, b, quad[:, b, 0:T])
            pe.wait_ge(sem("g_ready"), 1)
            pe.wait_ge(sem("v_act"), 1)
            pe.wait_ge(sem("v_dve"), 1)
            convolve(0, gl, 0, range(2), first=True)
            pe.wait_ge(sem("v_act"), 3)
            convolve(0, gl, 0, range(2, B))
            convolve(1, gl, 0, first=True)
            pe.wait_ge(sem("u_low"), 1)
            for b in range(B):
                to_phases(1, b, quad[:, b // 2, (b % 2) * T:(b % 2) * T + T])
            convolve(0, gh, 0)
            convolve(1, gh, 0)
            pe.wait_ge(sem("v_act"), 4)
            pe.wait_ge(sem("v_dve"), 2)
            convolve(0, gh, 1, last=True)
            convolve(1, gh, 1, last=True)
            for half in range(2):
                pe.wait_ge(sem("stu"), half + 1)
                for a in range(PA):
                    begin = max(HT * half, PH * a)
                    for b in range(B):
                        mm = pe.matmul(chainB[32 * b:32 * b + 32, begin:HT * half + HT], ident[:, 32 * a:32 * a + 32],
                                       yb[:, b, begin - PH * a:HT * half + HT - PH * a],
                                       start=False, stop=(a == PA - 1), skip_group_check=True)
            mm.then_inc(sem("back"), 1)

        @block.vector
        def _(dve):
            step = [0]

            def link(ins):
                step[0] += 1
                ins.then_inc(sem("dve_step"), 1)
                dve.wait_ge(sem("dve_step"), step[0])

            def mark(ins):
                step[0] += 1
                ins.then_inc(sem("dve_step"), 1)

            def settle():
                dve.wait_ge(sem("dve_step"), step[0])

            def g_low(q):
                dve.wait_ge(sem(f"g_high{q}"), 1)
                dve.tensor_tensor(gl[:, :, EG * q:EG * q + EG].rearrange("p m e -> p e m"),
                                  gacc[q].rearrange("p (e m) -> p e m", e=EG),
                                  gh[:, :, EG * q:EG * q + EG].rearrange("p m e -> p e m"),
                                  ALU.subtract).then_inc(sem(f"g_low{q}"), 1)

            def g_high1():
                dve.wait_ge(sem("g_psum"), 2)
                dve.tensor_copy(gh[:, :, EG:2 * EG].rearrange("p m e -> p e m"),
                                gacc[1].rearrange("p (e m) -> p e m", e=EG)).then_inc(sem("g_high1"), 1)

            def mst_low(n):
                dve.wait_ge(sem("mst_high"), n + 1)
                lower = mst[P // 2:P, 16 * n:16 * n + 16, :].rearrange("p e d -> p (e d)")
                dve.tensor_tensor(lower, mixbank[n][P // 2:P, :], lower, ALU.subtract).then_inc(sem("mst_low"), 1)

            def block_of(b):
                r = slice(32 * b, 32 * b + 32)
                dve.tensor_copy(blk[r, b, :], h[r, :]).then_inc(sem("blk_v"), 1)

            for n, v in enumerate((GN_EPS, BN_EPS, LN_EPS, LN_EPS * USCALE ** -2)):
                ins = dve.memset(eps[:, n:n + 1], v)
            ins.then_inc(sem("eps"), 1)
            dve.memset(busy[:, :], 1.0).then_inc(sem("busy"), 1)
            dve.wait_ge(sem("x_in"), 16)
            link(dve.bn_stats(rs6[:, :], x_sb[:, :]))
            dve.bn_aggr(st[:, 0:2], rs6[:, :]).then_inc(sem("gn_mv"), 1)
            dve.wait_ge(sem("gn_std"), 1)
            link(dve.reciprocal(grstd, gstd))
            dve.tensor_scalar(h[:, :], x_sb[:, :], mean, grstd, ALU.subtract, ALU.mult).then_inc(sem("h"), 1)
            dve.wait_ge(sem("h"), 1)
            dve.wait_ge(sem("zero"), 1)
            block_of(0)
            dve.wait_ge(sem("small_in"), 16)
            mark(dve.tensor_tensor(logits, sml[:, P_LOGW:P_LOGW + NX], sml[:, P_GUMBEL:P_GUMBEL + NX], ALU.add))
            dve.wait_ge(sem("hsq"), 1)
            dve.wait_ge(sem("hsq_high"), 1)
            dve.tensor_tensor(hq[:, 1, :], hsq[:, :], hq[:, 0, :], ALU.subtract).then_inc(sem("hsq_low"), 1)
            settle()
            mark(dve.reduce_max(lmax, logits, AX_X))
            block_of(1)
            settle()
            dve.tensor_scalar(ranked, logits, lmax, None, ALU.subtract).then_inc(sem("logits"), 1)
            dve.wait_ge(sem("phi_in"), 16)
            dve.tensor_reduce(amaxp[:, :], phi_sb[:, :], AX_X, ALU.max, apply_absolute_value=True)\
               .then_inc(sem("amaxp"), 1)
            dve.wait_ge(sem("m_in"), 16)
            mark(dve.tensor_reduce(rowmax[:, :], m_sb[:, :], AX_X, ALU.max, apply_absolute_value=True))
            dve.wait_ge(sem("mu_in"), 16)
            mark(dve.tensor_reduce(mumax[:, :], mu_sb[:, :, :], AX_X, ALU.max, apply_absolute_value=True))
            dve.wait_ge(sem("gmaxp"), 1)
            mark(dve.tensor_scalar(bnd, gmaxp[:, :], TINY, None, ALU.max))
            dve.wait_ge(sem("sqi_psum"), 1)
            dve.tensor_scalar(thr[:, :, :].rearrange("p h b -> p (h b)"), gbank[0][:, 0:2 * B], -1.0, -RADIUS2 / 2,
                              ALU.mult, ALU.add).then_inc(sem("thr"), 1)
            settle()
            mark(dve.tensor_scalar(p2_phi.bitcast(I32), bnd.bitcast(I32), 0x7F800000, None, ALU.bitwise_and))


            def compare(b, n):
                dve.wait_ge(sem("gram"), b + 1)
                if b < 2:
                    ins = dve.tensor_scalar(hgraph[:, b, n, :], quad[:, b, n * T:(n + 1) * T], thr[:, n, b:b + 1],
                                            0.0, ALU.is_gt, ALU.add, accum_out=deg[:, n, b:b + 1])
                else:
                    dve.wait_ge(sem("sqj"), 1)
                    ins = dve.scalar_tensor_tensor(out=hgraph[:, b, n, :], in0=quad[:, b, n * T:(n + 1) * T],
                                                   scalar=thr[:, n, b:b + 1], in1=sqj[:, b - 2, :],
                                                   op0=ALU.subtract, op1=ALU.is_gt, accum_out=deg[:, n, b:b + 1])
                ins.then_inc(sem("compare"), 1)

            dve.wait_ge(sem("thr"), 1)
            compare(0, 0)
            settle()
            mark(dve.reciprocal(sc_phi, p2_phi))
            dve.wait_ge(sem("expl"), 1)
            mark(dve.reciprocal(lrec, lsum))
            compare(0, 1)
            settle()
            dve.tensor_scalar(sc_phi, sc_phi, PTOP / 2, None, ALU.mult).then_inc(sem("scale_phi"), 1)
            mark(dve.tensor_scalar(soft, expl, lrec, None, ALU.mult))
            settle()
            mark(dve.reduce_max(smax, soft, AX_X))
            compare(1, 0)
            settle()
            mark(dve.scalar_tensor_tensor(out=ranked, in0=soft, scalar=smax, in1=sml[:, P_RANK:P_RANK + NX],
                                          op0=ALU.is_equal, op1=ALU.mult))
            compare(1, 1)
            settle()
            mark(dve.reduce_max(fmax, ranked, AX_X))
            compare(2, 0)
            settle()
            dve.tensor_scalar(onehot, ranked, fmax, None, ALU.is_equal).then_inc(sem("onehot"), 1)
            mark(dve.scalar_tensor_tensor(out=wts, in0=ranked, scalar=fmax, in1=soft,
                                          op0=ALU.is_equal, op1=ALU.subtract))
            compare(2, 1)
            settle()
            dve.tensor_tensor(wts, wts, soft, ALU.add).then_inc(sem("wts"), 1)
            compare(3, 0)
            compare(3, 1)
            dve.wait_ge(sem("wts"), 1)
            dve.wait_ge(sem("sig"), 2)
            settle()
            mark(dve.scalar_tensor_tensor(out=wsum[:, 0, :], in0=wts, scalar=sig, in1=sml[:, P_EXPERT:P_EXPERT + NX],
                                          op0=ALU.mult, op1=ALU.mult, accum_out=ws))
            dve.scalar_tensor_tensor(out=wsum[:, 1, :], in0=wts, scalar=1.0, in1=mumax[:, :],
                                     op0=ALU.mult, op1=ALU.mult, accum_out=amaxm[:, 1:2]).then_inc(sem("amaxm"), 1)
            settle()
            dve.tensor_scalar(amaxm[:, 0:1], rowmax[:, :], ws, TINY, ALU.mult, ALU.max).then_inc(sem("amaxm"), 1)
            dve.wait_ge(sem("compare"), 2 * B)
            dve.reciprocal(rdeg[:, :, :], deg[:, :, :]).then_inc(sem("rdeg"), 1)
            dve.wait_ge(sem("gmaxm"), 1)
            mark(dve.tensor_tensor(bnd, gmaxm[:, 1:2], sc_phi, ALU.mult))
            dve.wait_ge(sem("rdeg"), 1)
            dve.wait_ge(sem("edget_psum"), 1)
            dve.tensor_tensor(edget[:, :, :, :], chainB[:, 0:T].rearrange("p (h b c) -> p h b c", h=2, b=B),
                              rdeg[:, :, :].unsqueeze(3).broadcast_to([P, 2, B, C]), ALU.mult)\
               .then_inc(sem("edget"), 1)
            settle()
            link(dve.scalar_tensor_tensor(out=bnd, in0=bnd, scalar=1.0 / (16.0 * PTOP), in1=gmaxm[:, 0:1],
                                          op0=ALU.mult, op1=ALU.max))
            link(dve.tensor_scalar(p2_m.bitcast(I32), bnd.bitcast(I32), 0x7F800000, None, ALU.bitwise_and))
            link(dve.reciprocal(sc_m, p2_m))
            link(dve.scalar_tensor_tensor(out=ws, in0=sc_m, scalar=PTOP / 2, in1=ws, op0=ALU.mult, op1=ALU.mult))
            dve.wait_ge(sem("const_in"), 16)
            dve.tensor_scalar(rw[:, :], cst[:, REP_K:REP_K + P], ws, None, ALU.mult).then_inc(sem("rw"), 1)
            mark(dve.tensor_tensor(isc, p2_m, p2_phi, ALU.mult))
            dve.tensor_scalar(sc_m, sc_m, PTOP / 2, None, ALU.mult).then_inc(sem("scale_m"), 1)
            settle()
            dve.tensor_scalar(isc, isc, 4.0 / PTOP ** 2 / USCALE, None, ALU.mult).then_inc(sem("scale_m"), 1)
            dve.wait_ge(sem("vert_psum"), 1)
            dve.wait_ge(sem("rdegc"), 1)
            dve.tensor_tensor(conv[:, :], quad[:, 0, 0:T], rdegc[:, :], ALU.mult).then_inc(sem("vert"), 1)
            dve.wait_ge(sem("vert"), 1)
            dve.wait_ge(sem("hb"), 1)
            link(dve.tensor_tensor(conv[:, :], conv[:, :], hb[:, :], ALU.add))
            link(dve.bn_stats(cs6[:, :], conv[:, :]))
            dve.tensor_tensor(bnst[:, :, :], cst[:, BMASK:BMASK + B * 6].rearrange("p (b s) -> p b s", b=B),
                              cs6[:, :].unsqueeze(1).broadcast_to([P, B, 6]), ALU.mult).then_inc(sem("bnst"), 1)
            mst_low(0)
            dve.wait_ge(sem("bn_psum"), 1)
            dve.bn_aggr(bnaff[:, 0:2], chainB[:, 0:B * 6]).then_inc(sem("bn_mv"), 1)
            mark(dve.tensor_scalar(gamma2, sml[:, P_GAMMA:P_GAMMA + 1], 0.5, None, ALU.mult))
            mark(dve.tensor_scalar(beta2, sml[:, P_BETA:P_BETA + 1], 0.5, None, ALU.mult))
            mst_low(1)
            dve.wait_ge(sem("bn_mv"), 1)
            mark(dve.tensor_scalar(nmean, bnaff[:, 0:1], -1.0, None, ALU.mult))
            dve.wait_ge(sem("bn_std"), 1)
            link(dve.reciprocal(brstd, bstd))
            link(dve.tensor_tensor(ba2, brstd, gamma2, ALU.mult))
            dve.scalar_tensor_tensor(out=bb2, in0=ba2, scalar=nmean, in1=beta2, op0=ALU.mult, op1=ALU.add)\
               .then_inc(sem("halves"), 1)
            dve.wait_ge(sem("halves"), 1)
            dve.tensor_scalar(y[:, :], conv[:, :], ba2, bb2, ALU.mult, ALU.add).then_inc(sem("y"), 1)
            dve.wait_ge(sem("y"), 1)
            dve.wait_ge(sem("th"), 1)
            dve.scalar_tensor_tensor(out=silu[:, :], in0=th[:, :], scalar=1.0, in1=y[:, :],
                                     op0=ALU.add, op1=ALU.mult).then_inc(sem("silu"), 1)
            dve.wait_ge(sem("silu"), 1)
            dve.tensor_tensor(x1[:, :], silu[:, :], x_sb[:, :], ALU.add).then_inc(sem("x1"), 1)
            g_high1()
            dve.wait_ge(sem("sq"), 1)
            dve.tensor_copy(xm[:, :], quad[:, 0, 0:T]).then_inc(sem("xm"), 1)
            g_low(1)
            dve.wait_ge(sem("std"), 1)
            dve.reciprocal(rstd[:, :], std[:, :]).then_inc(sem("rstd"), 1)
            g_low(0)
            dve.wait_ge(sem("xm"), 1)
            dve.wait_ge(sem("rstdc_psum"), 1)
            dve.tensor_tensor(z[:, :], xm[:, :], chainA[:, 0:T], ALU.mult).then_inc(sem("z"), 1)
            g_low(2)
            g_low(3)
            dve.wait_ge(sem("exp"), 2 * B)
            dve.reciprocal(rstd[:, :], den[:, :, :].rearrange("p h b -> p (h b)")).then_inc(sem("rstd"), 1)
            dve.wait_ge(sem("o"), 1)
            dve.wait_ge(sem("rden_psum"), 1)
            dve.tensor_tensor(wo[:, :], chainB[:, 0:T], o_sb[:, :], ALU.mult).then_inc(sem("wo"), 1)
            dve.wait_ge(sem("wo"), 1)
            dve.tensor_tensor(t2[:, :], wo[:, :], x1[:, :], ALU.add).then_inc(sem("t2"), 1)
            dve.wait_ge(sem("sq"), 2)
            dve.tensor_copy(xm[:, :], quad[:, 0, 0:T]).then_inc(sem("xm"), 1)
            dve.wait_ge(sem("std"), 2)
            dve.reciprocal(rstd[:, :], std[:, :]).then_inc(sem("rstd"), 1)
            dve.wait_ge(sem("xm"), 2)
            dve.wait_ge(sem("rstdc_psum"), 2)
            uh, ul = (u2[:, n, PAD:PAD + T] for n in range(2))
            dve.tensor_tensor(uh, xm[:, :], chainA[:, 0:T], ALU.mult).then_inc(sem("u_high"), 1)
            mark(dve.tensor_tensor(u32[:, :], xm[:, :], chainA[:, 0:T], ALU.mult))
            dve.wait_ge(sem("v_psum"), 2)
            dve.tensor_copy(v2[:, 0, 1, :], quad[:, 1, 0:T]).then_inc(sem("v_dve"), 1)
            settle()
            dve.tensor_tensor(ul, u32[:, :], uh, ALU.subtract).then_inc(sem("u_low"), 1)
            dve.wait_ge(sem("v_psum"), 8)
            dve.tensor_copy(v2[:, 1, 2:4, :], quad[:, 1, :].rearrange("p (b t) -> p b t", b=2))\
               .then_inc(sem("v_dve"), 1)
            dve.wait_ge(sem("mask"), NX + PA)
            for half in range(2):
                t = slice(HT * half, HT * half + HT)
                dve.wait_ge(sem("stu_psum"), half + 1)
                dve.tensor_tensor(yb[:, :, t], gbank[half].rearrange("p (b t) -> p b t", b=B),
                                  maskp[:, t].unsqueeze(1).broadcast_to([P, B, HT]), ALU.mult).then_inc(sem("stu"), 1)
            dve.wait_ge(sem("back"), 1)
            dve.tensor_copy(res[:, :], chainB[:, 0:T]).then_inc(sem("res"), 1)


def constants():
    p = np.arange(P)
    group, chan = p // C, p % C
    same_group = group[:, None] == group[None, :]
    same_chan = chan[:, None] == chan[None, :]
    k = p % K
    minus = (p // K) % 2
    c = np.zeros((P, NCONST))
    c[:, IDENT:IDENT + P] = np.eye(P)
    c[:, CENTER:CENTER + P] = (same_chan - 1.0 / C) * same_group
    c[:, SAME_C:SAME_C + P] = same_chan
    c[:, REP_K:REP_K + P] = (k[:, None] == k[None, :]) & (minus[:, None] == minus[None, :])
    c[:, SIGN] = 1.0
    c[:, SIGN + 1] = 1.0 - 2.0 * minus
    c[:, COL32:COL32 + B] = (group[:, None] == np.arange(B)) / C
    c[:, BMASK:BMASK + B * 6] = np.repeat(group[:, None] == np.arange(B), 6, axis=1)
    return c.astype(np.float32)


def kernel(x, L0_conv_W_fc, L0_conv_b_fc, L0_conv_gamma, L0_conv_beta, L1_ffn_sigma, L1_ffn_phi, L1_ffn_M_u,
           L1_ffn_M_phi_plus, L1_ffn_M_phi_minus, L1_ffn_log_weights, L1_ffn_gumbel):
    import concourse.bacc as bacc
    from concourse.bass_utils import run_bass_kernel_spmd

    as_np = np.asarray
    small = np.zeros((P, NSMALL), np.float32)
    for b in range(B):
        small[32 * b:32 * b + 32, P_WT + 32 * b:P_WT + 32 * b + 32] = as_np(L0_conv_W_fc).T
    small[:, P_BIAS] = np.tile(as_np(L0_conv_b_fc), B)
    small[:, P_GAMMA] = np.tile(as_np(L0_conv_gamma), B)
    small[:, P_BETA] = np.tile(as_np(L0_conv_beta), B)
    small[:, P_SIGMA] = np.tile(as_np(L1_ffn_sigma), P // K)
    small[:, P_LOGW:P_LOGW + NX] = as_np(L1_ffn_log_weights)
    small[:, P_GUMBEL:P_GUMBEL + NX] = as_np(L1_ffn_gumbel)
    small[:, P_EXPERT:P_EXPERT + NX] = np.repeat(np.eye(NX), P // NX, axis=0)
    small[:, P_RANK:P_RANK + NX] = np.arange(NX, 0, -1)
    mfilt = np.stack([as_np(L1_ffn_M_phi_plus), as_np(L1_ffn_M_phi_minus)], 1).transpose(0, 1, 2, 4, 3)
    phi4 = np.tile(as_np(L1_ffn_phi)[:T].T, (P // K, 1))
    mu = as_np(L1_ffn_M_u)
    mu4 = np.zeros((PH, C, NX, C), np.float32)
    mu4[:NTAU] = mu.transpose(1, 2, 0, 3)

    ins = {
        "in_x": np.ascontiguousarray(as_np(x)).reshape(P, T),
        "in_consts": constants(),
        "in_small": small,
        "in_mfilt": np.ascontiguousarray(mfilt).reshape(P, C * C),
        "in_phi": np.ascontiguousarray(phi4),
        "in_mu": mu4.reshape(P, NX * C),
    }
    nc = bacc.Bacc("TRN2", target_bir_lowering=False, num_devices=1)
    aps = [nc.dram_tensor(n, a.shape, mybir.dt.from_np(a.dtype), kind="ExternalInput").ap() for n, a in ins.items()]
    out = nc.dram_tensor("out", (P, T), F32, kind="ExternalOutput").ap()
    stu_hybrid_kernel(nc, *aps, out)
    r = run_bass_kernel_spmd(nc, [ins], core_ids=[0])
    return r.results[0]["out"].reshape(B, C, 16, 16)
```
